# Optimizing a Trainium2 kernel written in Bass

```python
import numpy as np
import jax
import jax.numpy as jnp

def _softmax(x, axis=-1):
    return jax.nn.softmax(x, axis=axis)

def _gelu(x):
    return jax.nn.gelu(x, approximate=True)

def _silu(x):
    return jax.nn.silu(x)

def _sigmoid(x):
    return jax.nn.sigmoid(x)

def _layernorm(x, axis=-1, eps=1e-05):
    m = jnp.mean(x, axis=axis, keepdims=True)
    v = jnp.var(x, axis=axis, keepdims=True)
    return (x - m) / jnp.sqrt(v + eps)

def _scatter_add(tgt, idx, src, axis=0):
    return tgt.at[idx].add(src)

def _segment_sum(src, seg, n):
    return jax.ops.segment_sum(src, seg, n)
kernel_name = 'mk_flamingo_gated_d1_seqx_r8_77eb4d'

def setup_inputs(seed: int=0):
    np.random.seed(seed)
    _w = jnp.asarray

    def _rec_inputs():
        import jax
        import jax.numpy as jnp
        _rk = jax.random.key(seed)
        x = 7.22e-05 + 1 * jax.random.normal(jax.random.fold_in(_rk, 1), (8, 256, 128), jnp.float32)
        _lenS = 256 - jax.random.randint(jax.random.fold_in(_rk, 7), (8,), 0, max(1, 256 // 4) + 1, jnp.int32)
        _lenS2 = 256 - jax.random.randint(jax.random.fold_in(_rk, 8), (8,), 0, max(1, 256 // 4) + 1, jnp.int32)
        _ctx_1024P = jax.random.normal(jax.random.fold_in(_rk, 11), (8, 16, 128), jnp.float32)
        _ctx_1024c = jax.random.dirichlet(jax.random.fold_in(_rk, 511), 0.3 * jnp.ones((16,), jnp.float32), (8, 256))
        _ctx_1024t = jnp.einsum('bsk,bkd->bsd', _ctx_1024c, _ctx_1024P)
        _ctx_1024t = _ctx_1024t * jax.lax.rsqrt(jnp.mean(jnp.square(_ctx_1024t)) + 1e-12) * 0.953939
        ctx_1024 = 4.13588e-05 + 0.999923 * (_ctx_1024t + 0.3 * jax.random.normal(jax.random.fold_in(_rk, 611), (8, 256, 128), jnp.float32))
        _g = jax.random.normal(jax.random.fold_in(_rk, 9001), (2, 1), jnp.float32)
        _g = jnp.sign(_g) * jnp.maximum(jnp.abs(_g), 1.0) + (_g == 0) * 1.0
        g_xattn = _g[0]
        g_ffn = _g[1]
        return (x, ctx_1024, g_xattn, g_ffn)
    x, ctx_1024, g_xattn, g_ffn = _rec_inputs()

    def _L0_xattn_setup():
        import jax, jax.numpy as jnp
        import numpy as np
        H = 16
        D_MODEL = 128
        D_K = D_MODEL // H

        def _split_heads(x, B, T):
            return x.reshape(B, T, H, D_K).transpose(0, 2, 1, 3)
        key = jax.random.key(seed)
        ks = jax.random.split(key, 11)
        B, T = (4, 256)
        s = 1.0 / np.sqrt(D_MODEL)
        inp = {'query': jax.random.normal(ks[0], (B, T, D_MODEL), jnp.float32), 'key': jax.random.normal(ks[1], (B, T, D_MODEL), jnp.float32), 'value': jax.random.normal(ks[2], (B, T, D_MODEL), jnp.float32), 'Wq': jax.random.normal(ks[3], (D_MODEL, D_MODEL), jnp.float32) * s, 'bq': jnp.zeros((D_MODEL,), jnp.float32), 'Wk': jax.random.normal(ks[4], (D_MODEL, D_MODEL), jnp.float32) * s, 'bk': jnp.zeros((D_MODEL,), jnp.float32), 'Wv': jax.random.normal(ks[5], (D_MODEL, D_MODEL), jnp.float32) * s, 'bv': jnp.zeros((D_MODEL,), jnp.float32), 'Wo': jax.random.normal(ks[6], (D_MODEL, D_MODEL), jnp.float32) * s, 'bo': jnp.zeros((D_MODEL,), jnp.float32)}
        return inp
    _L0_xattn_all = _L0_xattn_setup()
    _L0_xattn_in = {k: v for k, v in _L0_xattn_all.items() if k in ('Wq', 'bq', 'Wk', 'bk', 'Wv', 'bv', 'Wo', 'bo')}
    del _L0_xattn_all

    def _L0_ffn_setup():
        import jax, jax.numpy as jnp
        import numpy as np
        DIM = 128
        DEPTH = 6
        HEADS = 16
        DIM_HEAD = 64
        WINDOW = 32
        INNER = HEADS * DIM_HEAD
        DIM_INNER = int(DIM * 4 * 2 / 3)
        QK_SCALE = 8.0

        def shift_tokens(t):
            a, s = jnp.split(t, 2, -1)
            s = jnp.pad(s, ((0, 0), (1, 0), (0, 0)))[:, :-1]
            return jnp.concatenate([a, s], -1)

        def l2norm(t):
            return t / jnp.maximum(jnp.linalg.norm(t, axis=-1, keepdims=True), 1e-12)

        def rotate_half(x):
            x1, x2 = jnp.split(x, 2, -1)
            return jnp.concatenate([-x2, x1], -1)

        def rotary_tables(n):
            half = jnp.arange(0, DIM_HEAD, 2, dtype=jnp.float32)
            inv_freq = 1.0 / 10000.0 ** (half / DIM_HEAD)
            t = jnp.arange(n, dtype=jnp.float32)
            freqs = t[:, None] * inv_freq[None, :]
            freqs = jnp.concatenate([freqs, freqs], -1)
            base_scale = (half + 0.4 * DIM_HEAD) / (1.4 * DIM_HEAD)
            power = (t - n // 2) / (WINDOW // 2)
            scale = base_scale[None, :] ** power[:, None]
            scale = jnp.concatenate([scale, scale], -1)
            return (freqs, scale)

        def local_attention(q, k, v):
            b, h, n, d = q.shape
            w = WINDOW
            nw = n // w
            bq = q.reshape(b, h, nw, w, d)
            bk = k.reshape(b, h, nw, w, d)
            bv = v.reshape(b, h, nw, w, d)

            def look(t):
                p = jnp.pad(t, ((0, 0), (0, 0), (1, 0), (0, 0), (0, 0)))
                return jnp.concatenate([p[:, :, :nw], p[:, :, 1:]], axis=3)
            bk2, bv2 = (look(bk), look(bv))
            seq = jnp.arange(n).reshape(nw, w)
            seq_p = jnp.pad(seq, ((1, 0), (0, 0)), constant_values=-1)
            jt = jnp.concatenate([seq_p[:nw], seq_p[1:]], axis=1)
            it = seq[:, :, None]
            jb = jt[:, None, :]
            mask = (it < jb) | (it > jb + w) | (jb == -1)
            sim = jnp.einsum('bhwie,bhwje->bhwij', bq, bk2) * QK_SCALE
            sim = jnp.where(mask, -jnp.finfo(sim.dtype).max, sim)
            attn = jax.nn.softmax(sim, -1)
            out = jnp.einsum('bhwij,bhwje->bhwie', attn, bv2)
            return out.reshape(b, h, n, d)

        def attn_layer(x, Wqkv, qs, ksc, Wo):
            b, n, _ = x.shape
            qkv = x @ Wqkv
            q, k, v = jnp.split(qkv, 3, -1)
            sh = lambda t: t.reshape(b, n, HEADS, DIM_HEAD).transpose(0, 2, 1, 3)
            q, k, v = (sh(q), sh(k), sh(v))
            q = l2norm(q) * qs
            k = l2norm(k) * ksc
            freqs, scale = rotary_tables(n)
            cos, sin = (jnp.cos(freqs), jnp.sin(freqs))
            q = q * cos * scale + rotate_half(q) * sin * scale
            inv = 1.0 / scale
            k = k * cos * inv + rotate_half(k) * sin * inv
            out = local_attention(q, k, v)
            out = out.transpose(0, 2, 1, 3).reshape(b, n, INNER)
            return out @ Wo

        def ffn_layer(x, g, bln, W1, b1, W2, b2):
            mu = x.mean(-1, keepdims=True)
            var = ((x - mu) ** 2).mean(-1, keepdims=True)
            xn = (x - mu) / jnp.sqrt(var + 1e-05) * g + bln
            hg = xn @ W1 + b1
            a, gate = jnp.split(hg, 2, -1)
            return a * jax.nn.gelu(gate, approximate=False) @ W2 + b2
        key = jax.random.key(seed)
        ks = jax.random.split(key, 8)
        B, N = (2, 256)
        init = lambda k, shape: jax.random.normal(k, shape, jnp.float32) * 0.02
        return {'x': jax.random.normal(ks[0], (B, N, DIM), jnp.float32), 'Wqkv': init(ks[1], (DEPTH, DIM, 3 * INNER)), 'q_scale': jnp.ones((DEPTH, DIM_HEAD), jnp.float32), 'k_scale': jnp.ones((DEPTH, DIM_HEAD), jnp.float32), 'Wo': init(ks[2], (DEPTH, INNER, DIM)), 'ln_g': jnp.ones((DEPTH, DIM), jnp.float32), 'ln_b': jnp.zeros((DEPTH, DIM), jnp.float32), 'W1': init(ks[3], (DEPTH, DIM, 2 * DIM_INNER)), 'b1': jnp.zeros((DEPTH, 2 * DIM_INNER), jnp.float32), 'W2': init(ks[4], (DEPTH, DIM_INNER, DIM)), 'b2': jnp.zeros((DEPTH, DIM), jnp.float32)}
    _L0_ffn_all = _L0_ffn_setup()
    _L0_ffn_in = {k: v for k, v in _L0_ffn_all.items() if k in ('Wqkv', 'q_scale', 'k_scale', 'Wo', 'ln_g', 'ln_b', 'W1', 'b1', 'W2', 'b2')}
    del _L0_ffn_all
    return {'x': x, 'ctx_1024': ctx_1024, 'g_xattn': g_xattn, 'g_ffn': g_ffn, 'L0_xattn_Wq': _L0_xattn_in['Wq'], 'L0_xattn_bq': _L0_xattn_in['bq'], 'L0_xattn_Wk': _L0_xattn_in['Wk'], 'L0_xattn_bk': _L0_xattn_in['bk'], 'L0_xattn_Wv': _L0_xattn_in['Wv'], 'L0_xattn_bv': _L0_xattn_in['bv'], 'L0_xattn_Wo': _L0_xattn_in['Wo'], 'L0_xattn_bo': _L0_xattn_in['bo'], 'L0_ffn_Wqkv': _L0_ffn_in['Wqkv'], 'L0_ffn_q_scale': _L0_ffn_in['q_scale'], 'L0_ffn_k_scale': _L0_ffn_in['k_scale'], 'L0_ffn_Wo': _L0_ffn_in['Wo'], 'L0_ffn_ln_g': _L0_ffn_in['ln_g'], 'L0_ffn_ln_b': _L0_ffn_in['ln_b'], 'L0_ffn_W1': _L0_ffn_in['W1'], 'L0_ffn_b1': _L0_ffn_in['b1'], 'L0_ffn_W2': _L0_ffn_in['W2'], 'L0_ffn_b2': _L0_ffn_in['b2']}

def reference(x, ctx_1024, g_xattn, g_ffn, L0_xattn_Wq, L0_xattn_bq, L0_xattn_Wk, L0_xattn_bk, L0_xattn_Wv, L0_xattn_bv, L0_xattn_Wo, L0_xattn_bo, L0_ffn_Wqkv, L0_ffn_q_scale, L0_ffn_k_scale, L0_ffn_Wo, L0_ffn_ln_g, L0_ffn_ln_b, L0_ffn_W1, L0_ffn_b1, L0_ffn_W2, L0_ffn_b2):
    import jax
    import jax.numpy as jnp

    def _L0_xattn_ref(query, key, value, Wq, bq, Wk, bk, Wv, bv, Wo, bo):
        import jax, jax.numpy as jnp
        import numpy as np
        H = 16
        D_MODEL = 128
        D_K = D_MODEL // H

        def _split_heads(x, B, T):
            return x.reshape(B, T, H, D_K).transpose(0, 2, 1, 3)
        B, T, _ = query.shape
        q = _split_heads(query @ Wq.T + bq, B, T)
        k = _split_heads(key @ Wk.T + bk, B, key.shape[1])
        v = _split_heads(value @ Wv.T + bv, B, value.shape[1])
        scores = jnp.einsum('bhqd,bhkd->bhqk', q, k) / jnp.sqrt(jnp.float32(D_K)).astype(q.dtype)
        weights = jax.nn.softmax(scores, axis=-1)
        x = jnp.einsum('bhqk,bhkd->bhqd', weights, v)
        x = x.transpose(0, 2, 1, 3).reshape(B, T, H * D_K)
        return x @ Wo.T + bo

    def _L0_ffn_ref(x, Wqkv, q_scale, k_scale, Wo, ln_g, ln_b, W1, b1, W2, b2):
        import jax, jax.numpy as jnp
        import numpy as np
        DIM = 128
        DEPTH = 6
        HEADS = 16
        DIM_HEAD = 64
        WINDOW = 32
        INNER = HEADS * DIM_HEAD
        DIM_INNER = int(DIM * 4 * 2 / 3)
        QK_SCALE = 8.0

        def shift_tokens(t):
            a, s = jnp.split(t, 2, -1)
            s = jnp.pad(s, ((0, 0), (1, 0), (0, 0)))[:, :-1]
            return jnp.concatenate([a, s], -1)

        def l2norm(t):
            return t / jnp.maximum(jnp.linalg.norm(t, axis=-1, keepdims=True), 1e-12)

        def rotate_half(x):
            x1, x2 = jnp.split(x, 2, -1)
            return jnp.concatenate([-x2, x1], -1)

        def rotary_tables(n):
            half = jnp.arange(0, DIM_HEAD, 2, dtype=jnp.float32)
            inv_freq = 1.0 / 10000.0 ** (half / DIM_HEAD)
            t = jnp.arange(n, dtype=jnp.float32)
            freqs = t[:, None] * inv_freq[None, :]
            freqs = jnp.concatenate([freqs, freqs], -1)
            base_scale = (half + 0.4 * DIM_HEAD) / (1.4 * DIM_HEAD)
            power = (t - n // 2) / (WINDOW // 2)
            scale = base_scale[None, :] ** power[:, None]
            scale = jnp.concatenate([scale, scale], -1)
            return (freqs, scale)

        def local_attention(q, k, v):
            b, h, n, d = q.shape
            w = WINDOW
            nw = n // w
            bq = q.reshape(b, h, nw, w, d)
            bk = k.reshape(b, h, nw, w, d)
            bv = v.reshape(b, h, nw, w, d)

            def look(t):
                p = jnp.pad(t, ((0, 0), (0, 0), (1, 0), (0, 0), (0, 0)))
                return jnp.concatenate([p[:, :, :nw], p[:, :, 1:]], axis=3)
            bk2, bv2 = (look(bk), look(bv))
            seq = jnp.arange(n).reshape(nw, w)
            seq_p = jnp.pad(seq, ((1, 0), (0, 0)), constant_values=-1)
            jt = jnp.concatenate([seq_p[:nw], seq_p[1:]], axis=1)
            it = seq[:, :, None]
            jb = jt[:, None, :]
            mask = (it < jb) | (it > jb + w) | (jb == -1)
            sim = jnp.einsum('bhwie,bhwje->bhwij', bq, bk2) * QK_SCALE
            sim = jnp.where(mask, -jnp.finfo(sim.dtype).max, sim)
            attn = jax.nn.softmax(sim, -1)
            out = jnp.einsum('bhwij,bhwje->bhwie', attn, bv2)
            return out.reshape(b, h, n, d)

        def attn_layer(x, Wqkv, qs, ksc, Wo):
            b, n, _ = x.shape
            qkv = x @ Wqkv
            q, k, v = jnp.split(qkv, 3, -1)
            sh = lambda t: t.reshape(b, n, HEADS, DIM_HEAD).transpose(0, 2, 1, 3)
            q, k, v = (sh(q), sh(k), sh(v))
            q = l2norm(q) * qs
            k = l2norm(k) * ksc
            freqs, scale = rotary_tables(n)
            cos, sin = (jnp.cos(freqs), jnp.sin(freqs))
            q = q * cos * scale + rotate_half(q) * sin * scale
            inv = 1.0 / scale
            k = k * cos * inv + rotate_half(k) * sin * inv
            out = local_attention(q, k, v)
            out = out.transpose(0, 2, 1, 3).reshape(b, n, INNER)
            return out @ Wo

        def ffn_layer(x, g, bln, W1, b1, W2, b2):
            mu = x.mean(-1, keepdims=True)
            var = ((x - mu) ** 2).mean(-1, keepdims=True)
            xn = (x - mu) / jnp.sqrt(var + 1e-05) * g + bln
            hg = xn @ W1 + b1
            a, gate = jnp.split(hg, 2, -1)
            return a * jax.nn.gelu(gate, approximate=False) @ W2 + b2
        for i in range(DEPTH):
            x = attn_layer(shift_tokens(x), Wqkv[i], q_scale[i], k_scale[i], Wo[i]) + x
            x = ffn_layer(shift_tokens(x), ln_g[i], ln_b[i], W1[i], b1[i], W2[i], b2[i]) + x
        return x
    x = x + jnp.tanh(g_xattn[0]) * _L0_xattn_ref(_layernorm(x, axis=-1), ctx_1024, ctx_1024, L0_xattn_Wq, L0_xattn_bq, L0_xattn_Wk, L0_xattn_bk, L0_xattn_Wv, L0_xattn_bv, L0_xattn_Wo, L0_xattn_bo)
    x = x + jnp.tanh(g_ffn[0]) * _L0_ffn_ref(_layernorm(x, axis=-1), L0_ffn_Wqkv, L0_ffn_q_scale, L0_ffn_k_scale, L0_ffn_Wo, L0_ffn_ln_g, L0_ffn_ln_b, L0_ffn_W1, L0_ffn_b1, L0_ffn_W2, L0_ffn_b2)
    return x

_drawn_inputs = setup_inputs


def setup_inputs(seed=0):
    import zlib

    import numpy as np

    out = dict(_drawn_inputs(seed))
    spreads = {'L0_xattn_bq': (0.0, 0.449),
     'L0_xattn_bk': (0.0, 0.8),
     'L0_xattn_bv': (0.0, 0.1),
     'L0_xattn_bo': (0.0, 0.1),
     'L0_ffn_q_scale': (1.0, 0.2),
     'L0_ffn_k_scale': (1.0, 0.2),
     'L0_ffn_ln_g': (1.0, 0.6),
     'L0_ffn_ln_b': (0.0, 0.745),
     'L0_ffn_b1': (0.0, 0.1),
     'L0_ffn_b2': (0.0, 0.1)}
    factors = {}
    for name, (base, spread) in spreads.items():
        noise = np.random.default_rng([zlib.crc32(name.encode()), seed]).standard_normal(out[name].shape)
        drawn = base * np.exp(spread * noise) if base else spread * noise
        out[name] = jnp.asarray(drawn.astype(out[name].dtype))
    for name, factor in factors.items():
        out[name] = (out[name] * factor).astype(out[name].dtype)
    return out
```

```python
from contextlib import ExitStack

import numpy as np
import concourse.bass as bass
from concourse import mybir

F32 = mybir.dt.float32
BF16 = mybir.dt.bfloat16
ALU = mybir.AluOpType
ACT = mybir.ActivationFunctionType
AX = mybir.AxisListType

P = 128
B, T = 8, 256
NT = T // P
L = 6
H = 16
XD = P // H
D = 64
INNER = H * D
PAIRS = H // 2
UNITS = 2 * PAIRS
WIN = 32
QW = P + WIN
HID = 341
HC = [(0, 128), (128, 128), (256, 85)]
NV = 13
CH = 4
CW = 512
MASKED = -1.0e30
FREE = 1
EPS = 1e-5


def shape_constants():
    f = np.float32
    half = np.arange(0, D, 2, dtype=f)
    inv_freq = (f(1.0) / (f(10000.0) ** (half / f(D)))).astype(f)
    t = np.arange(T, dtype=f)
    fr = (t[:, None] * inv_freq[None, :]).astype(f)
    base = ((half + f(0.4 * D)) / f(1.4 * D)).astype(f)
    scale = (base[None, :] ** ((t - T // 2) / f(WIN // 2))[:, None]).astype(f)
    cos, sin = np.cos(fr).T, np.sin(fr).T
    scale = scale.T
    sign = np.concatenate([-sin, sin])
    both = lambda a: np.concatenate([a, a])
    cq, sq = both(cos * scale), sign * both(scale)
    ck, sk = both(cos / scale), sign / both(scale)
    rot = np.stack([8.0 * both(cq), 8.0 * both(sq), both(ck), both(sk)], 1).astype(f)
    k, q = np.arange(P)[:, None], np.arange(QW)[None, :]
    seen = ((q // WIN == k // WIN) & (q >= k)) | ((q // WIN == k // WIN + 1) & (q <= k + WIN))
    mask_t = np.where(seen, 0.0, MASKED).astype(f)
    qq, kk = np.arange(P)[:, None], np.arange(QW)[None, :] - WIN
    seen = ((qq // WIN == kk // WIN) & (qq >= kk)) | ((qq // WIN == kk // WIN + 1) & (qq <= kk + WIN))
    mask_s = np.where(seen, 0.0, MASKED).astype(f)
    p = np.arange(P)
    sumsel = np.zeros((P, PAIRS, 32), f)
    for j in range(PAIRS):
        sumsel[p, j, 2 * j + p // D] = 1
    rsel = np.zeros((64, UNITS, P), f)
    for u in range(UNITS):
        rsel[32 * (u // PAIRS) + 2 * (u % PAIRS) + p // D, u, p] = 1
    densel = np.zeros((P, 4, 32), f)
    for j in range(4):
        densel[:, j, j::4] = 1
    rdsel = np.zeros((P, PAIRS, P), f)
    for j in range(PAIRS):
        h = 2 * j + p // D
        rdsel[32 * (h % 4) + h // 4, j, p] = 1
    xones = np.zeros((P, 4, 32), f)
    for j in range(4):
        xones[:, j, XD * j:XD * j + XD] = 1
    onehot = np.zeros((H, H, P), f)
    onehot[np.arange(H), np.arange(H), :] = 1
    hmask = np.zeros((P, H), f)
    hmask[p, p // XD] = 1
    flat = lambda a: a.reshape(a.shape[0], -1)
    c128 = np.concatenate([np.eye(P, dtype=f), np.full((P, P), 1.0 / P, f), flat(sumsel), flat(densel),
                           flat(xones), hmask, flat(rdsel), mask_t, mask_s], 1)
    return {"c_rot": flat(rot), "c_sel": np.ascontiguousarray(c128), "c_rsel": flat(rsel),
            "c_onehot": flat(onehot)}


C_PARTS = [("ident", P), ("mean", P), ("sumsel", PAIRS * 32), ("densel", 128), ("xones", 128),
           ("hmask", H), ("rdsel", PAIRS * P), ("mask_t", QW), ("mask_s", QW)]


def gated_flamingo(nc, x, ctx_in, xw, xvec, wn, wp, wo, w1, w2, vec, c_rot, c_sel, c_rsel, c_onehot, out):
    with ExitStack() as st:
        def sb(name, shape, dt=F32):
            return st.enter_context(nc.sbuf_tensor(name, shape, dt))

        def sem(name):
            return st.enter_context(nc.semaphore(name))

        width = sum(w for _, w in C_PARTS)
        sel = sb("sel", [P, width])
        part, at = {}, 0
        for name, w in C_PARTS:
            part[name] = sel[:, at:at + w]
            at += w
        ident, mean_w, hmask = part["ident"], part["mean"], part["hmask"]
        sumsel = part["sumsel"].rearrange("p (j m) -> p j m", j=PAIRS)
        densel = part["densel"].rearrange("p (j m) -> p j m", j=4)
        xones = part["xones"].rearrange("p (j m) -> p j m", j=4)
        rdsel = part["rdsel"].rearrange("p (j m) -> p j m", j=PAIRS)
        rot_base = sb("rot_base", [P, 4, T])
        rsel = sb("rsel", [64, UNITS, P])
        onehot_f = sb("onehot_f", [H, H * P])
        onehot = sb("onehot", [H, H, P], BF16)
        ident_b = sb("ident_b", [P, P], BF16)
        mask_tb = sb("mask_tb", [P, QW], BF16)
        mask_sb = sb("mask_sb", [P, QW], BF16)
        eps_col = sb("eps_col", [P, 1])
        x1 = sb("x1", [P, B, T])
        xs = sb("xs", [P, B, T + 1])
        xw_sb = sb("xw_sb", [P, 4, P])
        xv = sb("xv", [P, 6])
        gates = sb("gates", [P, 2])
        big = sb("big", [P, 22 * 1024])
        used = [0]

        def view(cols, *shape, dt=F32):
            a = big[:, used[0]:used[0] + cols]
            used[0] += cols
            if dt == BF16:
                a = a.bitcast(BF16)
            names = "abcd"[:len(shape)]
            return a.rearrange(f"p ({' '.join(names)}) -> p {' '.join(names)}", **dict(zip(names, shape)))

        xtok = view(2 * P, NT, P)
        ctok = view(2 * P, NT, P)
        xhat = view(2 * P, NT, P)
        bst = sb("bst", [P, NT, 6])
        bag = sb("bag", [P, NT, 2])
        tv = sb("tv", [P, 5, NT])
        xhT = view(T, 1, T)[:, 0, :]
        cT = view(T, 1, T)[:, 0, :]
        qT = view(T, 1, T)[:, 0, :]
        kT = view(T, 1, T)[:, 0, :]
        kTb = view(T // 2, 1, T, dt=BF16)[:, 0, :]
        qpad = view(H * T, H, T)
        qpadb = view(H * T // 2, H, T, dt=BF16)
        vpad = view(NT * H * 32, NT, H, 32)
        xP = view(4 * 2 * T, 4, 2, T)
        xrd = view(T, 1, T)[:, 0, :]
        xo = view(T, 1, T)[:, 0, :]
        xo2 = view(T, 1, T)[:, 0, :]
        xproj = view(T, 1, T)[:, 0, :]
        assert used[0] <= 22 * 1024
        used[0] = 0
        sT = view(T, 1, T)[:, 0, :]
        sq = view(4 * T, 4, T)
        qc = view(2 * T, 2, T)
        ps_ = view(2 * T, 2, T)
        rot = view(UNITS * T, UNITS, T)
        hat = view(UNITS * T, UNITS, T)
        hatb = view(UNITS * T // 2, UNITS, T, dt=BF16)
        vs = view(NT * INNER, NT, INNER)
        pt = view(4 * (QW + P), 4, QW + P)
        osb = view(PAIRS * T, PAIRS, T)
        rden = view(T, 1, T)[:, 0, :]
        nrm = view(4 * T, 4, T)
        assert used[0] <= 22 * 1024
        used[0] = 0
        s2 = view(CH * CW, CH, CW)
        xc = view(CH * CW, CH, CW)
        sq2 = view(CH * CW, CH, CW)
        va = view(CH * CW, CH, CW)
        y0 = view(CH * CW, CH, CW)
        y1 = view(CH * CW, CH, CW)
        gel = view(3 * CW, 3, CW)
        uu = view(6 * CW, 6, CW)
        otok = view(2 * 2 * P, 2, 2, P)
        assert used[0] <= 22 * 1024

        mcol = sb("mcol", [P, NT, H])
        mrow = sb("mrow", [H, T], BF16)
        tab = sb("tab", [P, 4, T])
        vecs = sb("vecs", [P, L, NV])
        vc = sb("vc", [P, NV])
        wn_sb = sb("wn_sb", [P, 3 * INNER])
        wp_sb = sb("wp_sb", [P, 2 * INNER])
        wo_sb = sb("wo_sb", [P, PAIRS, P])
        w1_sb = sb("w1_sb", [P, 2 * HID])
        w2_sb = sb("w2_sb", [P, 3, P])
        ps = st.enter_context(nc.psum_tensor("ps", [P, 8, 512], F32))

        s_const, s_w, s_wo, s_wf, s_x = (sem(n) for n in ("s_const", "s_w", "s_wo", "s_wf", "s_x"))
        s_out = [sem("s_out0"), sem("s_out1")]
        cast, gate, zero = sem("cast"), sem("gate"), sem("zero")
        xst, xrs, xln, xhat_d, xtr, xev, xpr, xqk, xvp, xpad, xpadb, xs_d, xmax = (
            sem(n) for n in ("xst", "xrs", "xln", "xhat_d", "xtr", "xev", "xpr", "xqk", "xvp", "xpad", "xpadb", "xs_d", "xmax"))
        xmt, xmr, xsc, xex, xav, xrd_d, xo_d, xwo, xres = (
            sem(n) for n in ("xmt", "xmr", "xsc", "xex", "xav", "xrd_d", "xo_d", "xwo", "xres"))
        vcur, tabs, shifted, proj, sq_d, vev, rotm, radd, sums, ss_d, ln_d, y_d, r_d = (
            sem(n) for n in ("vcur", "tabs", "shifted", "proj", "sq_d", "vev", "rotm", "radd", "sums", "ss_d", "ln_d", "y_d", "r_d"))
        rb, hat_d, hatb_d, sc_d, max_d, mt_d, mr_d, st_d, ex_d, ov_d, oev, rden_d, rdb, on_d, wo_d, x_d = (
            sem(n) for n in ("rb", "hat_d", "hatb_d", "sc_d", "max_d", "mt_d", "mr_d", "st_d", "ex_d", "ov_d", "oev",
                             "rden_d", "rdb", "on_d", "wo_d", "x_d"))
        chain = sem("chain")
        nsh, nmean, nxc, nsq, nvar, nva, nln, ny, nxn, nt = (
            sem(n) for n in ("nsh", "nmean", "nxc", "nsq", "nvar", "nva", "nln", "ny", "nxn", "nt"))
        fh, fg, fu, fo, fx = (sem(n) for n in ("fh", "fg", "fu", "fo", "fx"))
        gx, tr_o, ev_o = sem("gx"), sem("tr_o"), sem("ev_o")

        xv_q, xv_k, xv_v, xv_o, g_x, g_f = (xv[:, i:i + 1] for i in range(6))
        x_tok = x.rearrange("(b n p) d -> b p n d", b=B, p=P)
        c_tok = ctx_in.rearrange("(b n p) d -> b p n d", b=B, p=P)
        o_tok = out.rearrange("(b n p) d -> b p n d", b=B, p=P)
        hd = [4 * (i % 4) + i // 4 for i in range(H)]
        NORMS = L + 1

        block = st.enter_context(nc.Block())

        @block.sync
        def _(eng):
            eng.dma_start(sel[:, :], c_sel).then_inc(s_const, 16)
            eng.dma_start(onehot_f[:, :], c_onehot).then_inc(s_const, 16)
            eng.dma_start(xw_sb[:, :, :], xw).then_inc(s_const, 16)
            eng.dma_start(xv[:, :], xvec).then_inc(s_const, 16)
            eng.dma_start(rsel[:, :, :].rearrange("p a b -> p (a b)"), c_rsel).then_inc(s_const, 16)
            eng.dma_start(rot_base[:, :, :].rearrange("p a b -> p (a b)"), c_rot).then_inc(s_const, 16)
            eng.dma_start(vecs[:, :, :], vec).then_inc(s_const, 16)
            with eng.Fori(0, B) as b:
                eng.wait_ge(xtr, b * 6 + FREE)
                eng.dma_start(xtok, x_tok[bass.ds(b, 1)].rearrange("a p n d -> p (a n) d")).then_inc(s_x, 16)
                eng.dma_start(ctok, c_tok[bass.ds(b, 1)].rearrange("a p n d -> p (a n) d")).then_inc(s_x, 16)
            with eng.Fori(0, L) as l:
                eng.wait_ge(proj, l * (B * (UNITS + 4)) + FREE)
                eng.dma_start(wn_sb[:, :], wn[bass.ds(l, 1)].rearrange("a p n -> p (a n)")).then_inc(s_w, 16)
                eng.dma_start(wp_sb[:, :], wp[bass.ds(l, 1)].rearrange("a p n -> p (a n)")).then_inc(s_w, 16)
                eng.wait_ge(wo_d, l * B + FREE)
                eng.dma_start(wo_sb[:, :, :], wo[bass.ds(l, 1)].rearrange("a p j n -> p (a j) n")).then_inc(s_wo, 16)
                eng.wait_ge(fo, l * CH + FREE)
                eng.dma_start(w1_sb[:, :], w1[bass.ds(l, 1)].rearrange("a p n -> p (a n)")).then_inc(s_wf, 16)
                eng.dma_start(w2_sb[:, :, :], w2[bass.ds(l, 1)].rearrange("a p j n -> p (a j) n")).then_inc(s_wf, 16)
            for b in range(B):
                eng.wait_ge(ev_o, b + 1)
                eng.dma_start(o_tok[b], otok[:, b % 2, :, :]).then_inc(s_out[b % 2], 16)
            for q in s_out:
                eng.wait_ge(q, 16 * (B // 2))

        @block.gpsimd
        def _(eng):
            eng.sem_inc(radd, FREE)
            eng.memset(vpad, 0.0).then_inc(zero, 1)
            eng.memset(xs[:, :, 0:1], 0.0).then_inc(zero, 1)
            eng.memset(eps_col[:, :], EPS).then_inc(zero, 1)
            eng.wait_ge(s_const, 16 * 7)
            eng.tensor_copy(ident_b[:, :], ident).then_inc(cast, 1)
            eng.tensor_copy(mask_tb[:, :], part["mask_t"]).then_inc(cast, 1)
            eng.tensor_copy(mask_sb[:, :], part["mask_s"]).then_inc(cast, 1)
            eng.tensor_copy(onehot[:, :, :], onehot_f[:, :].rearrange("h (a b) -> h a b", a=H)).then_inc(cast, 1)


            eng.wait_ge(zero, 3)
            with eng.Fori(0, L) as l:
                with eng.Fori(0, B) as b:
                    it = eng.snap(l * B + b)
                    eng.wait_ge(nxn, CH)
                    eng.wait_ge(fx, l * CH + FREE)
                    eng.wait_ge(proj, it * (UNITS + 4) + FREE)
                    eng.wait_ge(radd, it * UNITS + FREE)
                    for half, off in ((0, 1), (1, 0)):
                        rows = slice(64 * half, 64 * half + 64)
                        eng.tensor_copy(sT[rows, :].rearrange("p (a t) -> p a t", a=1),
                                        xs[rows, bass.ds(b, 1), off:off + T]).then_inc(shifted, 1)
                    eng.wait_ge(hat_d, it * PAIRS + FREE)
                    for u in range(UNITS):
                        eng.wait_ge(rotm, it * UNITS + u + 1)
                        eng.tensor_tensor(rot[:, u, :], qc[:, u % 2, :], ps_[:, u % 2, :], ALU.add).then_inc(radd, 1)

        @block.scalar
        def _(eng):
            eng.sem_inc(oev, FREE)
            eng.wait_ge(s_const, 16 * 7)
            eng.activation(gates[:, :], xv[:, 4:6], ACT.Tanh).then_inc(gate, 1)
            eng.preload_act_table_set("natural_log_exp_and_others")
            eng.wait_ge(zero, 3)
            with eng.Fori(0, B) as b:
                eng.wait_ge(xst, b + 1)
                eng.activation(tv[:, 1, :], tv[:, 0, :], ACT.Ln).then_inc(xln, 1)
                eng.wait_ge(xln, b * 2 + 1)
                eng.activation(tv[:, 2, :], tv[:, 1, :], ACT.Exp, scale=-0.5).then_inc(xln, 1)
                eng.wait_ge(xtr, b * 6 + 2 + FREE)
                eng.activation(x1[:, bass.ds(b, 1), :].rearrange("p a t -> p (a t)"), ps[:, 0, 0:T], ACT.Copy).then_inc(xev, 1)
                eng.wait_ge(xtr, b * 6 + 4 + FREE)
                eng.activation(cT, ps[:, 1, 0:T], ACT.Copy).then_inc(xev, 1)
                eng.wait_ge(xtr, b * 6 + 6 + FREE)
                eng.activation(xhT, ps[:, 2, 0:T], ACT.Copy).then_inc(xev, 1)
                eng.wait_ge(xqk, b * 2 + 2)
                eng.activation(kTb, kT, ACT.Copy).then_inc(xpadb, 1)
                for i in range(4):
                    eng.wait_ge(xpad, b * H + 4 * i + 4)
                    eng.activation(qpadb[:, 4 * i:4 * i + 4, :], qpad[:, 4 * i:4 * i + 4, :], ACT.Copy).then_inc(xpadb, 1)
                eng.wait_ge(xmt, b + 1)
                eng.activation(mrow[:, :], ps[0:H, 0, 0:T], ACT.Copy).then_inc(xmr, 1)
                for n in range(2 * PAIRS):
                    pr, kt = divmod(n, 2)
                    eng.wait_ge(xsc, b * 2 * PAIRS + n + 1)
                    if n >= 4:
                        eng.wait_ge(xav, b * PAIRS + (n - 4) // 2 + 1)
                    eng.activation(xP[:, n % 4, :, :], ps[:, 2 + n % 4, :].rearrange("p (a t) -> p a t", a=2),
                                   ACT.Exp).then_inc(xex, 1)

            def norm(k):
                for c in range(CH):
                    eng.wait_ge(nxc, k * CH + c + 1)
                    eng.activation(sq2[:, c, :], xc[:, c, :], ACT.Square).then_inc(nsq, 1)
                for c in range(CH):
                    eng.wait_ge(nva, k * CH + c + 1)
                    eng.activation(y0[:, c, :], va[:, c, :], ACT.Ln).then_inc(nln, 1)
                for c in range(CH):
                    eng.wait_ge(nln, k * CH + c + 1)
                    eng.activation(y0[:, c, :], y0[:, c, :], ACT.Exp, scale=-0.5).then_inc(ny, 1)

            norm(0)
            with eng.Fori(0, L) as l:
                eng.preload_act_table_set("natural_log_exp_and_others")
                with eng.Fori(0, B) as b:
                    it = eng.snap(l * B + b)
                    for u in range(UNITS):
                        eng.wait_ge(proj, it * (UNITS + 4) + u + 1 + FREE)
                        eng.wait_ge(sums, it * UNITS + max(0, u - 3) + FREE)
                        eng.activation(sq[:, u % 4, :], ps[:, u % 2, 0:T], ACT.Square).then_inc(sq_d, 1)
                    for j in range(4):
                        u = UNITS + j
                        eng.wait_ge(proj, it * (UNITS + 4) + u + 1 + FREE)
                        eng.activation(vs[:, j // 2, (j % 2) * 512:(j % 2) * 512 + 512], ps[:, u % 2, :],
                                       ACT.Copy).then_inc(vev, 1)
                    eng.wait_ge(ss_d, it + 1)
                    eng.activation(nrm[0:64, 1, :], nrm[0:64, 0, :], ACT.Ln, scale=65536.0).then_inc(ln_d, 1)
                    eng.wait_ge(ln_d, it + 1)
                    eng.activation(nrm[0:64, 2, :], nrm[0:64, 1, :], ACT.Exp, scale=-0.5).then_inc(y_d, 1)
                    for i in range(PAIRS):
                        eng.wait_ge(hat_d, it * PAIRS + i + 1 + FREE)
                        eng.activation(hatb[:, 2 * i:2 * i + 2, :], hat[:, 2 * i:2 * i + 2, :], ACT.Copy).then_inc(hatb_d, 1)
                    eng.wait_ge(mt_d, it + 1)
                    eng.activation(mrow[:, :], ps[0:H, 2, 0:T], ACT.Copy).then_inc(mr_d, 1)

                    def evict(p):
                        eng.wait_ge(ov_d, it * PAIRS + p + 1)
                        eng.activation(osb[:, p, :], ps[:, (7, 2)[p % 2], 0:T], ACT.Copy).then_inc(oev, 1)

                    for h in range(H):
                        eng.wait_ge(st_d, it * H + h + 1)
                        if h >= 4:
                            eng.wait_ge(ov_d, it * PAIRS + (h - 4) // 2 + 1)
                        eng.activation(pt[:, h % 4, :], ps[:, 5 + h % 2, 0:QW + P], ACT.Exp).then_inc(ex_d, 1)
                        if h % 2 and h >= 3:
                            evict((h - 3) // 2)
                    evict(PAIRS - 1)
                eng.wait_ge(x_d, l * B + B)
                for c in range(CH):
                    for half, off in ((0, 1), (1, 0)):
                        rows = slice(64 * half, 64 * half + 64)
                        eng.activation(s2[rows, c, :].rearrange("p (a t) -> p a t", a=2),
                                       xs[rows, 2 * c:2 * c + 2, off:off + T], ACT.Copy).then_inc(nsh, 1)
                norm(l + 1)
                for c in range(CH):
                    for j, (_, m) in enumerate(HC):
                        n = 3 * c + j
                        eng.wait_ge(fh, l * 12 + n + 1)
                        if n >= 3:
                            eng.wait_ge(fu, l * 12 + n - 2)
                        eng.activation(gel[0:m, n % 3, :], ps[0:m, 2 * (n % 3) + 1, :], ACT.Gelu,
                                       bias=vc[0:m, 9 + j:10 + j]).then_inc(fg, 1)
            for b in range(B):
                eng.wait_ge(tr_o, b + 1)
                if b >= 2:
                    eng.wait_ge(s_out[b % 2], 16 * (b // 2))
                eng.activation(otok[:, b % 2, :, :], ps[:, b % 2, 0:T].rearrange("p (n d) -> p n d", n=NT),
                               ACT.Copy).then_inc(ev_o, 1)

        @block.vector
        def _(eng):
            for s in (hat_d, xres, on_d, fx):
                eng.sem_inc(s, FREE)
            eng.wait_ge(s_const, 16 * 7)
            eng.wait_ge(zero, 3)
            with eng.Fori(0, B) as b:
                eng.wait_ge(s_x, b * 32 + 32)
                for n in range(NT):
                    eng.bn_stats(bst[:, n, :], xtok[:, n, :]).then_inc(chain, 1)
                PER = 13
                base = lambda c: b * PER + c
                eng.wait_ge(chain, base(2))
                eng.tensor_tensor(tv[:, 1, :], bst[:, :, 1], bst[:, :, 4], ALU.subtract).then_inc(chain, 1)
                eng.tensor_tensor(tv[:, 2, :], bst[:, :, 2], bst[:, :, 5], ALU.add).then_inc(chain, 1)
                eng.tensor_tensor(bag[:, 1, :], bst[:, :, 1], bst[:, :, 4], ALU.add).then_inc(chain, 1)
                eng.wait_ge(chain, base(5))
                eng.scalar_tensor_tensor(tv[:, 1, :], tv[:, 1, :], 0.25, tv[:, 1, :], ALU.mult, ALU.mult).then_inc(chain, 1)
                eng.tensor_scalar(tv[:, 2, :], tv[:, 2, :], 1.0 / P, EPS, ALU.mult, ALU.add).then_inc(chain, 1)
                eng.tensor_scalar(bag[:, 0, :], bag[:, 1, :], 0.5, None, ALU.mult).then_inc(chain, 1)
                eng.wait_ge(chain, base(8))
                eng.tensor_tensor(tv[:, 0, :], tv[:, 1, :], tv[:, 2, :], ALU.add).then_inc(xst, 1)
                eng.wait_ge(xln, b * 2 + 2)
                eng.tensor_tensor(tv[:, 3, :], tv[:, 2, :], tv[:, 2, :], ALU.mult).then_inc(chain, 1)
                eng.wait_ge(chain, base(9))
                eng.scalar_tensor_tensor(tv[:, 3, :], tv[:, 3, :], -0.5, tv[:, 0, :], ALU.mult, ALU.mult).then_inc(chain, 1)
                eng.wait_ge(chain, base(10))
                eng.scalar_tensor_tensor(tv[:, 4, :], tv[:, 3, :], 1.5, tv[:, 2, :], ALU.add, ALU.mult).then_inc(chain, 1)
                eng.wait_ge(chain, base(11))
                for n in range(NT):
                    eng.tensor_scalar(xhat[:, n, :], xtok[:, n, :], bag[:, 0, n:n + 1], tv[:, 4, n:n + 1],
                                      ALU.subtract, ALU.mult).then_inc(xhat_d, 1)
                eng.wait_ge(xpr, b * 4 + 1)
                eng.tensor_scalar(qT, ps[:, 3, 0:T], xv_q, float(np.float32(1) / np.sqrt(np.float32(XD))),
                                  ALU.add, ALU.mult).then_inc(xqk, 1)
                eng.wait_ge(xpr, b * 4 + 2)
                eng.tensor_scalar(kT, ps[:, 4, 0:T], xv_k, None, ALU.add).then_inc(xqk, 1)
                eng.wait_ge(xqk, b * 2 + 1)
                for i in range(H):
                    eng.tensor_scalar(qpad[:, i, :], qT, hmask[:, hd[i]:hd[i] + 1], None, ALU.mult).then_inc(xpad, 1)
                eng.wait_ge(xpr, b * 4 + 4)
                vsrc = ps[:, 5, 0:T].rearrange("p (n a j d) -> p n a j d", n=NT, a=4, j=4)
                vdst = vpad.rearrange("p n (a j) (m d) -> p n a j m d", j=4, m=4)
                for n in range(NT):
                    for j in range(4):
                        eng.tensor_copy(vdst[:, n, :, j, j, :], vsrc[:, n, :, j, :]).then_inc(xvp, 1)
                for n in range(NT * PAIRS):
                    t_, pr = divmod(n, PAIRS)
                    eng.wait_ge(xs_d, b * NT * PAIRS + n + 1)
                    eng.tensor_reduce(mcol[:, t_, 2 * pr:2 * pr + 2], ps[:, 6 + n % 2, :].rearrange("p (a t) -> p a t", a=2),
                                      AX.X, ALU.max, negate=True).then_inc(xmax, 1)
                eng.wait_ge(xav, b * PAIRS + PAIRS)
                eng.reciprocal(xrd, ps[:, 7, 0:T]).then_inc(xrd_d, 1)
                eng.wait_ge(xrd_d, b + 1)
                eng.tensor_tensor(xo, ps[:, 6, 0:T], xrd, ALU.mult).then_inc(chain, 1)
                eng.wait_ge(chain, base(12))
                eng.tensor_scalar(xo2, xo, xv_v, None, ALU.add).then_inc(xo_d, 1)
                eng.wait_ge(xwo, b + 1)
                eng.wait_ge(gate, 1)
                eng.tensor_scalar(xproj, ps[:, 0, 0:T], xv_o, gates[:, 0:1], ALU.add, ALU.mult).then_inc(chain, 1)
                eng.wait_ge(chain, base(13))
                x1b = x1[:, bass.ds(b, 1), :].rearrange("p a t -> p (a t)")
                eng.tensor_tensor(x1b, x1b, xproj, ALU.add).then_inc(xres, 1)

            def norm(k, src, dst, affine):
                for c in range(CH):
                    eng.wait_ge(nmean, k * CH + c + 1)
                    eng.tensor_tensor(xc[:, c, :], src(c), ps[:, c, :], ALU.subtract).then_inc(nxc, 1)
                for c in range(CH):
                    eng.wait_ge(nvar, k * CH + c + 1)
                    eng.tensor_scalar(va[:, c, :], ps[:, 4 + c, :], EPS, None, ALU.add).then_inc(nva, 1)
                steps = 3 + affine
                tb = lambda c, j: (CH * 3 + (k - 1) * CH * 4 if affine else 0) + j * CH + c + 1
                for c in range(CH):
                    eng.wait_ge(ny, k * CH + c + 1)
                    eng.tensor_tensor(y1[:, c, :], y0[:, c, :], y0[:, c, :], ALU.mult).then_inc(nt, 1)
                for c in range(CH):
                    eng.wait_ge(nt, tb(c, 0))
                    eng.scalar_tensor_tensor(y1[:, c, :], y1[:, c, :], -0.5, va[:, c, :], ALU.mult, ALU.mult).then_inc(nt, 1)
                for c in range(CH):
                    eng.wait_ge(nt, tb(c, 1))
                    eng.scalar_tensor_tensor(y1[:, c, :], y1[:, c, :], 1.5, y0[:, c, :], ALU.add, ALU.mult).then_inc(nt, 1)
                for c in range(CH):
                    eng.wait_ge(nt, tb(c, 2))
                    if affine:
                        eng.tensor_tensor(xc[:, c, :], xc[:, c, :], y1[:, c, :], ALU.mult).then_inc(nt, 1)
                        eng.wait_ge(nt, tb(c, 3))
                        eng.tensor_scalar(dst(c), xc[:, c, :], vc[:, 4:5], vc[:, 5:6], ALU.mult, ALU.add).then_inc(nxn, 1)
                    else:
                        eng.tensor_tensor(dst(c), xc[:, c, :].rearrange("p (a t) -> p a t", a=2),
                                          y1[:, c, :].rearrange("p (a t) -> p a t", a=2), ALU.mult).then_inc(nxn, 1)

            norm(0, lambda c: x1[:, 2 * c:2 * c + 2, :].rearrange("p a t -> p (a t)"),
                 lambda c: xs[:, 2 * c:2 * c + 2, 1:T + 1], 0)
            chain0 = B * 13
            with eng.Fori(0, L) as l:
                eng.wait_ge(fx, l * CH + FREE)
                eng.tensor_copy(vc[:, :], vecs[:, bass.ds(l, 1), :].rearrange("p a n -> p (a n)")).then_inc(vcur, 1)
                eng.wait_ge(vcur, l + 1)
                for i in range(4):
                    eng.tensor_scalar(tab[:, i, :], rot_base[:, i, :], vc[:, i:i + 1], None, ALU.mult).then_inc(tabs, 1)
                with eng.Fori(0, B) as b:
                    it = eng.snap(l * B + b)
                    eng.wait_ge(tabs, l * 4 + 4)
                    for u in range(UNITS):
                        k = u // PAIRS
                        eng.wait_ge(sq_d, it * UNITS + u + 1)
                        if u >= 2:
                            eng.wait_ge(radd, it * UNITS + u - 1 + FREE)
                        eng.tensor_tensor(qc[:, u % 2, :], ps[:, u % 2, 0:T], tab[:, 2 * k, :], ALU.mult)
                        eng.tensor_tensor(ps_[:, u % 2, :], ps[:, u % 2, T:2 * T], tab[:, 2 * k + 1, :],
                                          ALU.mult).then_inc(rotm, 1)
                    eng.wait_ge(sums, it * UNITS + UNITS + FREE)
                    eng.tensor_scalar(nrm[0:64, 0, :], ps[0:64, 2, 0:T], 1e-24, None, ALU.max).then_inc(ss_d, 1)
                    eng.wait_ge(y_d, it + 1)
                    cb = lambda c: it * 3 + (chain0 + c)
                    eng.tensor_scalar(nrm[0:64, 2, :], nrm[0:64, 2, :], 256.0, None, ALU.mult).then_inc(chain, 1)
                    eng.wait_ge(chain, cb(1))
                    eng.tensor_tensor(nrm[0:64, 1, :], nrm[0:64, 2, :], nrm[0:64, 2, :], ALU.mult).then_inc(chain, 1)
                    eng.wait_ge(chain, cb(2))
                    eng.scalar_tensor_tensor(nrm[0:64, 1, :], nrm[0:64, 1, :], -0.5, nrm[0:64, 0, :], ALU.mult,
                                             ALU.mult).then_inc(chain, 1)
                    eng.wait_ge(chain, cb(3))
                    eng.scalar_tensor_tensor(nrm[0:64, 3, :], nrm[0:64, 1, :], 1.5, nrm[0:64, 2, :], ALU.add,
                                             ALU.mult).then_inc(r_d, 1)
                    for i in range(PAIRS):
                        eng.wait_ge(rb, it * PAIRS + i + 1)
                        eng.wait_ge(radd, it * UNITS + 2 * i + 2 + FREE)
                        eng.tensor_tensor(hat[:, 2 * i:2 * i + 2, :], rot[:, 2 * i:2 * i + 2, :],
                                          ps[:, i % 2, :].rearrange("p (a t) -> p a t", a=2), ALU.mult).then_inc(hat_d, 1)
                    for h in range(H):
                        eng.wait_ge(sc_d, it * H + h + 1)
                        eng.tensor_reduce(mcol[:, 0, h:h + 1], ps[:, 3 + h % 2, 0:P], AX.X, ALU.max, negate=True)
                        eng.tensor_reduce(mcol[:, 1, h:h + 1], ps[:, 3 + h % 2, P:P + QW], AX.X, ALU.max,
                                          negate=True).then_inc(max_d, 1)
                    eng.wait_ge(ov_d, it * PAIRS + PAIRS)
                    eng.reciprocal(rden, ps[:, 3, 0:T]).then_inc(rden_d, 1)
                    for i in range(PAIRS // 2):
                        eng.wait_ge(rdb, it * 4 + i + 1)
                        eng.wait_ge(oev, it * PAIRS + 2 * i + 2 + FREE)
                        eng.tensor_tensor(osb[:, 2 * i:2 * i + 2, :], osb[:, 2 * i:2 * i + 2, :],
                                          ps[:, i % 2, :].rearrange("p (a t) -> p a t", a=2), ALU.mult).then_inc(on_d, 1)
                    eng.wait_ge(wo_d, it + 1 + FREE)
                    xb = xs[:, bass.ds(b, 1), 1:T + 1]
                    eng.tensor_tensor(xb, xb, ps[:, 4:5, 0:T], ALU.add).then_inc(x_d, 1)
                norm_l = l
                for c in range(CH):
                    eng.wait_ge(nmean, norm_l * CH + (CH + c + 1))
                    eng.wait_ge(nsh, norm_l * 8 + (2 * c + 2))
                    eng.tensor_tensor(xc[:, c, :], s2[:, c, :], ps[:, c, :], ALU.subtract).then_inc(nxc, 1)
                for c in range(CH):
                    eng.wait_ge(nvar, norm_l * CH + (CH + c + 1))
                    eng.tensor_scalar(va[:, c, :], ps[:, 4 + c, :], EPS, None, ALU.add).then_inc(nva, 1)
                tb = lambda c, j: norm_l * (4 * CH) + (3 * CH + j * CH + c + 1)
                for c in range(CH):
                    eng.wait_ge(ny, norm_l * CH + (CH + c + 1))
                    eng.tensor_tensor(y1[:, c, :], y0[:, c, :], y0[:, c, :], ALU.mult).then_inc(nt, 1)
                for c in range(CH):
                    eng.wait_ge(nt, tb(c, 0))
                    eng.scalar_tensor_tensor(y1[:, c, :], y1[:, c, :], -0.5, va[:, c, :], ALU.mult, ALU.mult).then_inc(nt, 1)
                for c in range(CH):
                    eng.wait_ge(nt, tb(c, 1))
                    eng.scalar_tensor_tensor(y1[:, c, :], y1[:, c, :], 1.5, y0[:, c, :], ALU.add, ALU.mult).then_inc(nt, 1)
                for c in range(CH):
                    eng.wait_ge(nt, tb(c, 2))
                    eng.tensor_tensor(xc[:, c, :], xc[:, c, :], y1[:, c, :], ALU.mult).then_inc(nt, 1)
                for c in range(CH):
                    eng.wait_ge(nt, tb(c, 3))
                    eng.tensor_scalar(s2[:, c, :], xc[:, c, :], vc[:, 4:5], vc[:, 5:6], ALU.mult, ALU.add).then_inc(nxn, 1)

                def residual(c):
                    eng.wait_ge(fo, l * CH + c + 1 + FREE)
                    xb = xs[:, 2 * c:2 * c + 2, 1:T + 1]
                    eng.scalar_tensor_tensor(xb, ps[:, 6 + c % 2, :].rearrange("p (a t) -> p a t", a=2), vc[:, 12:13], xb,
                                             ALU.add, ALU.add).then_inc(fx, 1)

                for c in range(CH):
                    for j, (_, m) in enumerate(HC):
                        n = 3 * c + j
                        eng.wait_ge(fg, l * 12 + n + 1)
                        eng.scalar_tensor_tensor(uu[0:m, n % 6, :], ps[0:m, 2 * (n % 3), :], vc[0:m, 6 + j:7 + j],
                                                 gel[0:m, n % 3, :], ALU.add, ALU.mult).then_inc(fu, 1)
                    if c:
                        residual(c - 1)
                residual(CH - 1)
            eng.wait_ge(fx, L * CH + FREE)
            for b in range(B):
                eng.scalar_tensor_tensor(x1[:, b, :], xs[:, b, 1:T + 1], gates[:, 1:2], x1[:, b, :], ALU.mult,
                                         ALU.add).then_inc(gx, 1)

        @block.tensor
        def _(eng):
            for s in (xtr, proj, sums, wo_d, fo):
                eng.sem_inc(s, FREE)
            eng.wait_ge(s_const, 16 * 7)
            eng.wait_ge(cast, 4)
            with eng.Fori(0, B) as b:
                eng.wait_ge(s_x, b * 32 + 32)
                eng.wait_ge(xres, b + FREE)
                for n in range(NT):
                    eng.transpose(ps[:, 0, n * P:n * P + P], xtok[:, n, :], ident).then_inc(xtr, 1)
                for n in range(NT):
                    eng.transpose(ps[:, 1, n * P:n * P + P], ctok[:, n, :], ident).then_inc(xtr, 1)
                for n in range(NT):
                    eng.wait_ge(xhat_d, b * NT + n + 1)
                    eng.transpose(ps[:, 2, n * P:n * P + P], xhat[:, n, :], ident).then_inc(xtr, 1)
                eng.wait_ge(xev, b * 3 + 3)
                eng.matmul(ps[:, 3, 0:T], xw_sb[:, 0, :], xhT, start=True, stop=True).then_inc(xpr, 1)
                eng.matmul(ps[:, 4, 0:T], xw_sb[:, 1, :], cT, start=True, stop=True).then_inc(xpr, 1)
                for n in range(NT):
                    eng.matmul(ps[:, 5, n * P:n * P + P], cT[:, n * P:n * P + P], xw_sb[:, 2, :],
                               start=True, stop=True).then_inc(xpr, 1)
                eng.wait_ge(xpadb, b * 5 + 5)
                for n in range(NT * PAIRS):
                    t_, pr = divmod(n, PAIRS)
                    if n >= 2:
                        eng.wait_ge(xmax, b * NT * PAIRS + n - 1)
                    for a in range(2):
                        mm = eng.matmul(ps[:, 6 + n % 2, a * T:a * T + T], qpadb[:, 2 * pr + a, t_ * P:t_ * P + P], kTb,
                                        start=True, stop=True)
                    mm.then_inc(xs_d, 1)
                eng.wait_ge(xmax, b * NT * PAIRS + NT * PAIRS)
                for n in range(NT):
                    mm = eng.transpose(ps[0:H, 0, n * P:n * P + P], mcol[:, n, :], ident)
                mm.then_inc(xmt, 1)
                eng.wait_ge(xvp, b * 8 + 8)

                def score(n):
                    pr, kt = divmod(n, 2)
                    if n >= 4:
                        eng.wait_ge(xex, b * 2 * PAIRS + n - 3)
                    bank = ps[:, 2 + n % 4, :]
                    eng.matmul(bank, kT[:, kt * P:kt * P + P], qpad[:, 2 * pr:2 * pr + 2, :].rearrange("p a t -> p (a t)"),
                               start=True, stop=False, skip_group_check=True)
                    if n == 0:
                        eng.wait_ge(xmr, b + 1)
                    for a in range(2):
                        mm = eng.matmul(bank[:, a * T:a * T + T], onehot[:, 2 * pr + a, :], mrow[:, :],
                                        start=False, stop=a == 1, skip_group_check=True)
                    mm.then_inc(xsc, 1)

                def weigh(pr):
                    eng.wait_ge(xex, b * 2 * PAIRS + 2 * pr + 2)
                    for kt in range(NT):
                        for bank in (6, 7):
                            for a in range(2):
                                h = hd[2 * pr + a]
                                g = h // 4
                                w = vpad[:, kt, h, :] if bank == 6 else xones[:, h % 4, :]
                                first = h % 4 == 0 and kt == 0
                                mm = eng.matmul(ps[32 * g:32 * g + 32, bank, 0:T], w, xP[:, (2 * pr + kt) % 4, a, :],
                                                start=first, stop=h % 4 == 3 and kt == 1, skip_group_check=True)
                    mm.then_inc(xav, 1)

                for pr in range(PAIRS):
                    score(2 * pr)
                    score(2 * pr + 1)
                    if pr:
                        weigh(pr - 1)
                weigh(PAIRS - 1)
                eng.wait_ge(xo_d, b + 1)
                eng.matmul(ps[:, 0, 0:T], xw_sb[:, 3, :], xo2, start=True, stop=True).then_inc(xwo, 1)

            eng.wait_ge(xres, B + FREE)
            for c in range(CH):
                eng.matmul(ps[:, c, :], mean_w, x1[:, 2 * c:2 * c + 2, :].rearrange("p a t -> p (a t)"),
                           start=True, stop=True).then_inc(nmean, 1)
            for c in range(CH):
                eng.wait_ge(nsq, c + 1)
                eng.matmul(ps[:, 4 + c, :], mean_w, sq2[:, c, :], start=True, stop=True).then_inc(nvar, 1)
            eng.wait_ge(nxn, CH)

            with eng.Fori(0, L) as l:
                with eng.Fori(0, B) as b:
                    it = eng.snap(l * B + b)
                    eng.wait_ge(s_w, l * 32 + 32)
                    eng.wait_ge(shifted, it * 2 + 2)
                    eng.wait_ge(oev, it * PAIRS + FREE)
                    eng.wait_ge(on_d, it * 4 + FREE)
                    eng.wait_ge(fx, l * CH + FREE)

                    def head_sums(u):
                        side, j = divmod(u, PAIRS)
                        eng.wait_ge(sq_d, it * UNITS + u + 1)
                        eng.matmul(ps[32 * side:32 * side + 32, 2, 0:T], sumsel[:, j, :], sq[:, u % 4, :],
                                   start=j == 0, stop=j == PAIRS - 1, skip_group_check=True).then_inc(sums, 1)

                    for u in range(UNITS):
                        if u >= 2:
                            eng.wait_ge(rotm, it * UNITS + u - 1)
                            eng.wait_ge(sq_d, it * UNITS + u - 1)
                        eng.matmul(ps[:, u % 2, 0:T], wn_sb[:, u * P:u * P + P], sT, start=True, stop=True)
                        eng.matmul(ps[:, u % 2, T:2 * T], wp_sb[:, u * P:u * P + P], sT, start=True,
                                   stop=True).then_inc(proj, 1)
                        if u >= 2:
                            head_sums(u - 2)
                    head_sums(UNITS - 2)
                    head_sums(UNITS - 1)
                    for j in range(4):
                        n, c = divmod(j, 2)
                        if j < 2:
                            eng.wait_ge(rotm, it * UNITS + UNITS - 1 + j)
                        else:
                            eng.wait_ge(vev, it * 4 + j - 1)
                        eng.matmul(ps[:, j % 2, :], sT[:, n * P:n * P + P], wn_sb[:, 2 * INNER + c * 512:2 * INNER + c * 512 + 512],
                                   start=True, stop=True).then_inc(proj, 1)
                    eng.wait_ge(r_d, it + 1)
                    for i in range(PAIRS):
                        if i < 2:
                            eng.wait_ge(vev, it * 4 + 3 + i)
                        else:
                            eng.wait_ge(hat_d, it * PAIRS + i - 1 + FREE)
                        for a in range(2):
                            mm = eng.matmul(ps[:, i % 2, a * T:a * T + T], rsel[:, 2 * i + a, :], nrm[0:64, 3, :],
                                            start=True, stop=True)
                        mm.then_inc(rb, 1)
                    for h in range(H):
                        p, r = divmod(h, 2)
                        rows = slice(64 * r, 64 * r + 64)
                        if r == 0:
                            eng.wait_ge(hatb_d, it * PAIRS + PAIRS // 2 + p // 2 + 1)
                        if h >= 2:
                            eng.wait_ge(max_d, it * H + h - 1)
                        bank = ps[:, 3 + r, :]
                        eng.matmul(bank[:, 0:P], ident_b[:, :], mask_sb[:, WIN:QW], start=True, stop=False)
                        eng.matmul(bank[:, 0:P], hatb[rows, p, 0:P], hatb[rows, PAIRS + p, 0:P], start=False, stop=True)
                        eng.matmul(bank[:, P:P + QW], ident_b[:, :], mask_sb[:, :], start=True, stop=False)
                        eng.matmul(bank[:, P:P + QW], hatb[rows, p, P:T], hatb[rows, PAIRS + p, P - WIN:T],
                                   start=False, stop=True).then_inc(sc_d, 1)
                    eng.wait_ge(max_d, it * H + H)
                    for n in range(NT):
                        mm = eng.transpose(ps[0:H, 2, n * P:n * P + P], mcol[:, n, :], ident)
                    mm.then_inc(mt_d, 1)

                    def score(h):
                        p, r = divmod(h, 2)
                        rows = slice(64 * r, 64 * r + 64)
                        if h >= 2:
                            eng.wait_ge(ex_d, it * H + h - 1)
                        bank = ps[:, 5 + r, :]
                        for n, (lo, w) in enumerate(((0, QW), (QW, P))):
                            o = bank[:, lo:lo + w]
                            q0 = n * P
                            eng.matmul(o, ident_b[:, :], mask_tb[:, 0:w], start=True, stop=False)
                            if h == 0 and n == 0:
                                eng.wait_ge(mr_d, it + 1)
                            eng.matmul(o, onehot[:, h, :], mrow[:, q0:q0 + w], start=False, stop=False)
                            mm = eng.matmul(o, hat[rows, PAIRS + p, n * P:n * P + P], hat[rows, p, q0:q0 + w],
                                            start=False, stop=True)
                        mm.then_inc(st_d, 1)

                    def weigh(p):
                        eng.wait_ge(ex_d, it * H + 2 * p + 2)
                        if p >= 2:
                            eng.wait_ge(oev, it * PAIRS + p - 1 + FREE)
                        for n, (lo, w) in enumerate(((0, QW), (QW, P))):
                            for r in range(2):
                                h = 2 * p + r
                                mm = eng.matmul(ps[64 * r:64 * r + 64, (7, 2)[p % 2], n * P:n * P + w],
                                                vs[:, n, h * D:h * D + D], pt[:, h % 4, lo:lo + w],
                                                start=n == 0, stop=n == 1, skip_group_check=True)
                        for n, (lo, w) in enumerate(((0, QW), (QW, P))):
                            for r in range(2):
                                h = 2 * p + r
                                g = h % 4
                                mm = eng.matmul(ps[32 * g:32 * g + 32, 3, n * P:n * P + w], densel[:, h // 4, :],
                                                pt[:, h % 4, lo:lo + w], start=h < 4 and n == 0,
                                                stop=h >= 12 and n == 1, skip_group_check=True)
                        mm.then_inc(ov_d, 1)

                    for p in range(PAIRS):
                        score(2 * p)
                        score(2 * p + 1)
                        if p:
                            weigh(p - 1)
                    weigh(PAIRS - 1)
                    eng.wait_ge(rden_d, it + 1)
                    for i in range(PAIRS // 2):
                        if i >= 2:
                            eng.wait_ge(on_d, it * 4 + i - 1 + FREE)
                        for a in range(2):
                            mm = eng.matmul(ps[:, i % 2, a * T:a * T + T], rdsel[:, 2 * i + a, :], rden, start=True, stop=True)
                        mm.then_inc(rdb, 1)
                    eng.wait_ge(s_wo, l * 16 + 16)
                    for p in range(PAIRS):
                        eng.wait_ge(on_d, it * 4 + p // 2 + 1 + FREE)
                        mm = eng.matmul(ps[:, 4, 0:T], wo_sb[:, p, :], osb[:, p, :], start=p == 0, stop=p == PAIRS - 1)
                    mm.then_inc(wo_d, 1)
                eng.wait_ge(x_d, l * B + B)
                for c in range(CH):
                    eng.wait_ge(nsh, l * 8 + (2 * c + 2))
                    eng.matmul(ps[:, c, :], mean_w, s2[:, c, :], start=True, stop=True).then_inc(nmean, 1)
                for c in range(CH):
                    eng.wait_ge(nsq, l * CH + (CH + c + 1))
                    eng.matmul(ps[:, 4 + c, :], mean_w, sq2[:, c, :], start=True, stop=True).then_inc(nvar, 1)
                eng.wait_ge(s_wf, l * 32 + 32)
                eng.wait_ge(nva, l * CH + 2 * CH)

                def down(c):
                    if c >= 2:
                        eng.wait_ge(fx, l * CH + c - 1 + FREE)
                    for j, (_, m) in enumerate(HC):
                        eng.wait_ge(fu, l * 12 + 3 * c + j + 1)
                        mm = eng.matmul(ps[:, 6 + c % 2, :], w2_sb[0:m, j, :], uu[0:m, (3 * c + j) % 6, :],
                                        start=j == 0, stop=j == 2)
                    mm.then_inc(fo, 1)

                for c in range(CH):
                    eng.wait_ge(nxn, l * CH + (CH + c + 1))
                    for j, (o, m) in enumerate(HC):
                        n = 3 * c + j
                        if n >= 3:
                            eng.wait_ge(fu, l * 12 + n - 2)
                        eng.matmul(ps[0:m, 2 * (n % 3), :], w1_sb[:, o:o + m], s2[:, c, :], start=True, stop=True)
                        eng.matmul(ps[0:m, 2 * (n % 3) + 1, :], w1_sb[:, HID + o:HID + o + m], s2[:, c, :], start=True,
                                   stop=True).then_inc(fh, 1)
                    if c:
                        down(c - 1)
                down(CH - 1)
            for b in range(B):
                eng.wait_ge(gx, b + 1)
                if b >= 2:
                    eng.wait_ge(ev_o, b - 1)
                for n in range(NT):
                    mm = eng.transpose(ps[:, b % 2, n * P:n * P + P], x1[:, b, n * P:n * P + P], ident)
                mm.then_inc(tr_o, 1)


def laid_out(inputs):
    a = {k: np.asarray(v) for k, v in inputs.items()}
    up = "L0_xattn_"
    fp = "L0_ffn_"
    wn = a[fp + "Wqkv"]
    swap = (np.arange(D) + D // 2) % D
    wp = wn[:, :, :2 * INNER].reshape(L, P, 2 * H, D)[..., swap].reshape(L, P, 2 * INNER)
    two = lambda v: np.concatenate([v, v], 1)
    b1 = a[fp + "b1"]
    vec = np.zeros((P, L, NV), np.float32)
    qs, ks = a[fp + "q_scale"], a[fp + "k_scale"]
    for i, v in enumerate([two(qs), two(qs[:, swap]), two(ks), two(ks[:, swap]), a[fp + "ln_g"], a[fp + "ln_b"]]):
        vec[:, :, i] = v.T
    for j, (o, m) in enumerate(HC):
        vec[:m, :, 6 + j] = b1[:, o:o + m].T
        vec[:m, :, 9 + j] = b1[:, HID + o:HID + o + m].T
    vec[:, :, 12] = a[fp + "b2"].T
    w2 = np.zeros((L, P, 3, P), np.float32)
    for j, (o, m) in enumerate(HC):
        w2[:, :m, j, :] = a[fp + "W2"][:, o:o + m, :]
    xw = np.stack([a[up + n].T for n in ("Wq", "Wk", "Wv", "Wo")], 1)
    wide = lambda v: np.broadcast_to(v, (P,))
    xvec = np.stack([a[up + "bq"], a[up + "bk"], a[up + "bv"], a[up + "bo"], wide(a["g_xattn"]), wide(a["g_ffn"])], 1)
    arrays = {
        "x": a["x"].reshape(B * T, P), "ctx": a["ctx_1024"].reshape(B * T, P), "xw": xw, "xvec": xvec,
        "wn": wn, "wp": wp, "wo": a[fp + "Wo"].reshape(L, PAIRS, P, P).transpose(0, 2, 1, 3), "w1": a[fp + "W1"],
        "w2": w2, "vec": vec,
    }
    arrays.update(shape_constants())
    return {k: np.ascontiguousarray(v) for k, v in arrays.items()}


def kernel(**inputs):
    import concourse.bacc as bacc
    from concourse.bass_utils import run_bass_kernel_spmd

    arrays = laid_out(inputs)
    nc = bacc.Bacc("TRN2", target_bir_lowering=False, num_devices=1)
    args = [nc.dram_tensor(f"in_{k}", v.shape, mybir.dt.from_np(v.dtype), kind="ExternalInput").ap()
            for k, v in arrays.items()]
    out = nc.dram_tensor("out_0", (B * T, P), F32, kind="ExternalOutput").ap()
    gated_flamingo(nc, *args, out)
    r = run_bass_kernel_spmd(nc, [{f"in_{k}": v for k, v in arrays.items()}], core_ids=[0])
    return r.results[0]["out_0"].reshape(B, T, P)
```

```python
from contextlib import ExitStack

import numpy as np
import concourse.bass as bass
from concourse import mybir

F32 = mybir.dt.float32
BF16 = mybir.dt.bfloat16
ALU = mybir.AluOpType
ACT = mybir.ActivationFunctionType
AX = mybir.AxisListType

P = 128
B, T = 8, 256
NT = T // P
L = 6
H = 16
XD = P // H
D = 64
INNER = H * D
PAIRS = H // 2
UNITS = 2 * PAIRS
WIN = 32
QW = P + WIN
HID = 341
HC = [(0, 128), (128, 128), (256, 85)]
NV = 13
CH = 4
CW = 512
MASKED = -1.0e30
FREE = 1
EPS = 1e-5
BIG = 26 * 1024


def shape_constants():
    f = np.float32
    half = np.arange(0, D, 2, dtype=f)
    inv_freq = (f(1.0) / (f(10000.0) ** (half / f(D)))).astype(f)
    t = np.arange(T, dtype=f)
    fr = (t[:, None] * inv_freq[None, :]).astype(f)
    base = ((half + f(0.4 * D)) / f(1.4 * D)).astype(f)
    scale = (base[None, :] ** ((t - T // 2) / f(WIN // 2))[:, None]).astype(f)
    cos, sin = np.cos(fr).T, np.sin(fr).T
    scale = scale.T
    sign = np.concatenate([-sin, sin])
    both = lambda a: np.concatenate([a, a])
    cq, sq = both(cos * scale), sign * both(scale)
    ck, sk = both(cos / scale), sign / both(scale)
    rot = np.stack([8.0 * both(cq), 8.0 * both(sq), both(ck), both(sk)], 1).astype(f)
    k, q = np.arange(P)[:, None], np.arange(QW)[None, :]
    seen = ((q // WIN == k // WIN) & (q >= k)) | ((q // WIN == k // WIN + 1) & (q <= k + WIN))
    mask_t = np.where(seen, 0.0, MASKED).astype(f)
    qq, kk = np.arange(P)[:, None], np.arange(QW)[None, :] - WIN
    seen = ((qq // WIN == kk // WIN) & (qq >= kk)) | ((qq // WIN == kk // WIN + 1) & (qq <= kk + WIN))
    mask_s = np.where(seen, 0.0, MASKED).astype(f)
    p = np.arange(P)
    m = p % 32
    sumsel = np.zeros((P, 4, 32), f)
    for j in range(4):
        for c in range(4):
            sumsel[p, j, 8 * c + 2 * j + p // D] = 1
    rsel = np.zeros((P, UNITS, P), f)
    for u in range(UNITS):
        for c in range(3):
            rsel[32 * (u % 4) + 8 * c + 2 * (u // 4) + p // D, u, p] = 1
    parts = -np.stack([(m // 8 >= 1) & (m < 24), m // 8 == 2, (m // 4 >= 1) & (m < 12), m // 4 == 2], 1).astype(f)
    densel = np.zeros((P, 4, 32), f)
    for j in range(4):
        densel[:, j, j::4] = 1
    rdsel = np.zeros((P, PAIRS, P), f)
    for j in range(PAIRS):
        h = 2 * j + p // D
        for c in range(3):
            rdsel[32 * (h % 4) + 4 * c + h // 4, j, p] = -1
    xones = np.zeros((P, 4, 32), f)
    for j in range(4):
        xones[:, j, XD * j:XD * j + XD] = 1
    onehot = np.zeros((H, H, P), f)
    onehot[np.arange(H), np.arange(H), :] = 1
    hmask = np.zeros((P, H), f)
    hmask[p, p // XD] = 1
    flat = lambda a: a.reshape(a.shape[0], -1)
    c128 = np.concatenate([np.eye(P, dtype=f), np.full((P, P), 1.0 / P, f), flat(sumsel), flat(densel),
                           flat(xones), hmask, parts, flat(rdsel), mask_t, mask_t[:, 0:P],
                           np.full((P, WIN), MASKED, f), mask_s[:, WIN:], mask_s], 1)
    return {"c_rot": flat(rot), "c_sel": np.ascontiguousarray(c128), "c_rsel": flat(rsel),
            "c_onehot": flat(onehot)}


C_PARTS = [("ident", P), ("mean", P), ("sumsel", 4 * 32), ("densel", 128), ("xones", 128),
           ("hmask", H), ("parts", 4), ("rdsel", PAIRS * P), ("mask_t", QW + P), ("mask_s", 2 * QW)]


def gated_flamingo(nc, x, ctx_in, xw, xvec, wn, wp, wo, w1, w2, vec, c_rot, c_sel, c_rsel, c_onehot, out):
    with ExitStack() as st:
        def sb(name, shape, dt=F32):
            return st.enter_context(nc.sbuf_tensor(name, shape, dt))

        def sem(name):
            return st.enter_context(nc.semaphore(name))

        width = sum(w for _, w in C_PARTS)
        sel = sb("sel", [P, width])
        part, at = {}, 0
        for name, w in C_PARTS:
            part[name] = sel[:, at:at + w]
            at += w
        ident, mean_w, hmask = part["ident"], part["mean"], part["hmask"]
        sumsel = part["sumsel"].rearrange("p (j m) -> p j m", j=4)
        densel = part["densel"].rearrange("p (j m) -> p j m", j=4)
        xones = part["xones"].rearrange("p (j m) -> p j m", j=4)
        rot_base = sb("rot_base", [P, 4, T])
        rselb = sb("rselb", [P, UNITS, P], BF16)
        rdselb = sb("rdselb", [P, PAIRS, P], BF16)
        onehot = sb("onehot", [H, H, P], BF16)
        ident_b = sb("ident_b", [P, P], BF16)
        mask_tb = sb("mask_tb", [P, QW + P], BF16)
        mask_sb = sb("mask_sb", [P, 2 * QW], BF16)
        zeros = sb("zeros", [P, 1, T])
        x1 = sb("x1", [P, B, T])
        xs = sb("xs", [P, B, T + 1])
        xw_sb = sb("xw_sb", [P, 4, P])
        xv = sb("xv", [P, 6])
        gates = sb("gates", [P, 2])
        big = sb("big", [P, BIG])
        used = [0]

        def view(cols, *shape, dt=F32):
            a = big[:, used[0]:used[0] + cols]
            used[0] += cols
            if dt == BF16:
                a = a.bitcast(BF16)
            names = "abcd"[:len(shape)]
            return a.rearrange(f"p ({' '.join(names)}) -> p {' '.join(names)}", **dict(zip(names, shape)))

        xtok = view(2 * P, NT, P)
        ctok = view(2 * P, NT, P)
        xhat = view(2 * P, NT, P)
        bst = sb("bst", [P, NT, 6])
        bag = sb("bag", [P, NT, 2])
        tv = sb("tv", [P, 5, NT])
        xhT = view(T, 1, T)[:, 0, :]
        cT = view(T, 1, T)[:, 0, :]
        qT = view(T, 1, T)[:, 0, :]
        kT = view(T, 1, T)[:, 0, :]
        kTb = view(T // 2, 1, T, dt=BF16)[:, 0, :]
        qpad = view(H * T, H, T)
        qpadb = view(H * T // 2, H, T, dt=BF16)
        vpad = view(NT * H * 32, NT, H, 32)
        xP = view(4 * 2 * T, 4, 2, T)
        xrd = view(T, 1, T)[:, 0, :]
        xo = view(T, 1, T)[:, 0, :]
        xo2 = view(T, 1, T)[:, 0, :]
        xproj = view(T, 1, T)[:, 0, :]
        assert used[0] <= BIG
        used[0] = 0
        xc0 = view(CH * CW, CH, CW)
        sq0 = view(CH * CW, CH, CW)
        va0 = view(CH * CW, CH, CW)
        z0 = view(CH * CW, CH, CW)
        z1 = view(CH * CW, CH, CW)
        assert used[0] <= BIG
        used[0] = 0
        one = lambda: view(T, 1, T)[:, 0, :]
        sT = one()
        sq = view(8 * T, 8, T)
        qc = view(2 * T, 2, T)
        ps_ = view(2 * T, 2, T)
        rot = view(UNITS * T, UNITS, T)
        hat = view(UNITS * T, UNITS, T)
        hatb = view(UNITS * T // 2, UNITS, T, dt=BF16)
        vs = view(NT * INNER, NT, INNER)
        pt = view(4 * (QW + P), 4, QW + P)
        osb = view(PAIRS * T, PAIRS, T)
        n_s, n_y, n_t, n_r, n_z = one(), one(), one(), one(), one()
        d_s, d_y, d_t, d_r, d_z = one(), one(), one(), one(), one()
        half = lambda: view(T // 2, 1, T, dt=BF16)[:, 0, :]
        n_hi, n_mid, n_parts, d_hi, d_mid, d_parts = half(), half(), half(), half(), half(), half()
        s2, xc, sq2, va, y0, y1, xn = one(), one(), one(), one(), one(), one(), one()
        gt = view(3 * T, 3, T)
        gel = view(3 * T, 3, T)
        a2 = one()
        uu = view(3 * T, 3, T)
        assert used[0] <= BIG
        used[0] = 0
        otok = view(2 * 2 * P, 2, 2, P)

        mcol = sb("mcol", [P, NT, H])
        mrow = sb("mrow", [H, QW + P], BF16)
        tab = sb("tab", [P, 4, T])
        vecs = sb("vecs", [P, L, NV])
        va_c = sb("va_c", [P, 4])
        vf = sb("vf", [P, NV])
        wn_sb = sb("wn_sb", [P, 3 * INNER])
        wp_sb = sb("wp_sb", [P, 2 * INNER])
        wo_sb = sb("wo_sb", [P, PAIRS, P])
        w1_sb = sb("w1_sb", [P, 2 * HID])
        w2_sb = sb("w2_sb", [P, 3, P])
        ps = st.enter_context(nc.psum_tensor("ps", [P, 8, 512], F32))

        s_const, s_w, s_wo, s_wf, s_x = (sem(n) for n in ("s_const", "s_w", "s_wo", "s_wf", "s_x"))
        s_out = [sem("s_out0"), sem("s_out1")]
        cast, gate, zero = sem("cast"), sem("gate"), sem("zero")
        xst, xrs, xln, xhat_d, xtr, xev, xpr, xqk, xvp, xpad, xpadb, xs_d, xmax = (
            sem(n) for n in ("xst", "xrs", "xln", "xhat_d", "xtr", "xev", "xpr", "xqk", "xvp", "xpad", "xpadb", "xs_d", "xmax"))
        xmt, xmr, xsc, xex, xav, xrd_d, xo_d, xwo, xres = (
            sem(n) for n in ("xmt", "xmr", "xsc", "xex", "xav", "xrd_d", "xo_d", "xwo", "xres"))
        vcur, tabs, shifted, proj, sq_d, vev, rotm, radd, sums, ss_d, ln_d, y_d, r_d = (
            sem(n) for n in ("vcur", "tabs", "shifted", "proj", "sq_d", "vev", "rotm", "radd", "sums", "ss_d", "ln_d", "y_d", "r_d"))
        rb, hat_d, hatb_d, sc_d, max_d, mt_d, mr_d = (
            sem(n) for n in ("rb", "hat_d", "hatb_d", "sc_d", "max_d", "mt_d", "mr_d"))
        st_d, ex_d, ov_d, oev, dev, dln, dy, dp, rdb, on_d, wo_d, x_d = (
            sem(n) for n in ("st_d", "ex_d", "ov_d", "oev", "dev", "dln", "dy", "dp", "rdb", "on_d", "wo_d", "x_d"))
        chain, nchain, nmid, dchain = sem("chain"), sem("nchain"), sem("nmid"), sem("dchain")
        nmean, nxc, nsq, nvar, nva, nln, ny, nxn, nt = (
            sem(n) for n in ("nmean", "nxc", "nsq", "nvar", "nva", "nln", "ny", "nxn", "nt"))
        fsh, fmean, fxc, fsq, fvar, fva, fln, fy, fchain, fxn = (
            sem(n) for n in ("fsh", "fmean", "fxc", "fsq", "fvar", "fva", "fln", "fy", "fchain", "fxn"))
        fh, fev, fg, fu, fo, fx, fvc = (sem(n) for n in ("fh", "fev", "fg", "fu", "fo", "fx", "fvc"))
        gx, tr_o, ev_o = sem("gx"), sem("tr_o"), sem("ev_o")

        xv_q, xv_k, xv_v, xv_o, g_x, g_f = (xv[:, i:i + 1] for i in range(6))
        CASTS = 6
        x_tok = x.rearrange("(b n p) d -> b p n d", b=B, p=P)
        c_tok = ctx_in.rearrange("(b n p) d -> b p n d", b=B, p=P)
        o_tok = out.rearrange("(b n p) d -> b p n d", b=B, p=P)
        hd = [4 * (i % 4) + i // 4 for i in range(H)]

        SLOTS = ["uuhuh", "uhuhu"] + ["uhuh"] * 5 + ["vhvh"]
        HATS = [i // 2 + PAIRS // 2 * (i % 2) for i in range(PAIRS)]
        steps = []
        u = h = v = 0
        for s_ in SLOTS:
            row = []
            for k_ in s_:
                row.append((k_, {"u": u, "h": h, "v": v}[k_]))
                u, h, v = u + (k_ == "u"), h + (k_ == "h"), v + (k_ == "v")
            steps.append(row)
        first_unit = [min([x_ for k_, x_ in row if k_ == "u"] + [UNITS]) for row in steps] + [UNITS]

        def seq(b, n):
            return slice((b - n) % B, (b - n) % B + 1) if isinstance(b, int) else bass.ds(b - n, 1)

        def pipeline(eng, body, layer_start=None, layer_second=None):
            def layer(l, first):
                if layer_start:
                    layer_start(l, first)
                body(0, eng.snap(l * B) if not first else 0, l, True, not first, not first, first)
                body(1, eng.snap(l * B + 1) if not first else 1, l, True, True, not first, first)
                if layer_second:
                    layer_second(l, first)
                with eng.Fori(2, B) as b:
                    body(b, eng.snap(l * B + b), l, True, True, True, first)
            layer(0, True)
            with eng.Fori(1, L) as l:
                layer(l, False)
            body(0, L * B, L, False, True, True, False)
            body(1, L * B + 1, L, False, False, True, False)

        block = st.enter_context(nc.Block())

        @block.sync
        def _(eng):
            eng.dma_start(sel[:, :], c_sel).then_inc(s_const, 16)
            eng.dma_start(wp_sb[0:H, 0:H * P], c_onehot).then_inc(s_const, 16)
            eng.dma_start(xw_sb[:, :, :], xw).then_inc(s_const, 16)
            eng.dma_start(xv[:, :], xvec).then_inc(s_const, 16)
            eng.dma_start(wn_sb[:, 0:UNITS * P], c_rsel).then_inc(s_const, 16)
            eng.dma_start(rot_base[:, :, :].rearrange("p a b -> p (a b)"), c_rot).then_inc(s_const, 16)
            eng.dma_start(vecs[:, :, :], vec).then_inc(s_const, 16)
            with eng.Fori(0, B) as b:
                eng.wait_ge(xtr, b * 6 + FREE)
                eng.dma_start(xtok, x_tok[bass.ds(b, 1)].rearrange("a p n d -> p (a n) d")).then_inc(s_x, 16)
                eng.dma_start(ctok, c_tok[bass.ds(b, 1)].rearrange("a p n d -> p (a n) d")).then_inc(s_x, 16)
            eng.wait_ge(cast, CASTS)
            with eng.Fori(0, L) as l:
                eng.wait_ge(proj, l * (B * (UNITS + 4)) + FREE)
                eng.dma_start(wn_sb[:, :], wn[bass.ds(l, 1)].rearrange("a p n -> p (a n)")).then_inc(s_w, 16)
                eng.dma_start(wp_sb[:, :], wp[bass.ds(l, 1)].rearrange("a p n -> p (a n)")).then_inc(s_w, 16)
                eng.wait_ge(wo_d, l * B + FREE)
                eng.dma_start(wo_sb[:, :, :], wo[bass.ds(l, 1)].rearrange("a p j n -> p (a j) n")).then_inc(s_wo, 16)
                eng.wait_ge(fo, l * B + FREE)
                eng.dma_start(w1_sb[:, :], w1[bass.ds(l, 1)].rearrange("a p n -> p (a n)")).then_inc(s_wf, 16)
                eng.dma_start(w2_sb[:, :, :], w2[bass.ds(l, 1)].rearrange("a p j n -> p (a j) n")).then_inc(s_wf, 16)
            for b in range(B):
                eng.wait_ge(ev_o, b + 1)
                eng.dma_start(o_tok[b], otok[:, b % 2, :, :]).then_inc(s_out[b % 2], 16)
            for q in s_out:
                eng.wait_ge(q, 16 * (B // 2))

        @block.gpsimd
        def _(eng):
            eng.sem_inc(radd, FREE)
            eng.memset(vpad, 0.0).then_inc(zero, 1)
            eng.memset(xs[:, :, 0:1], 0.0).then_inc(zero, 1)
            eng.memset(zeros[:, :, :], 0.0).then_inc(zero, 1)
            eng.wait_ge(s_const, 16 * 7)
            eng.tensor_copy(ident_b[:, :], ident).then_inc(cast, 1)
            eng.tensor_copy(mask_tb[:, :], part["mask_t"]).then_inc(cast, 1)
            eng.tensor_copy(mask_sb[:, :], part["mask_s"]).then_inc(cast, 1)
            eng.tensor_copy(onehot[:, :, :], wp_sb[0:H, 0:H * P].rearrange("h (a b) -> h a b", a=H)).then_inc(cast, 1)
            eng.tensor_copy(rselb[:, :, :].rearrange("p a b -> p (a b)"), wn_sb[:, 0:UNITS * P]).then_inc(cast, 1)
            eng.tensor_copy(rdselb[:, :, :].rearrange("p a b -> p (a b)"), part["rdsel"]).then_inc(cast, 1)
            eng.wait_ge(nxn, CH)
            eng.memset(gt[:, 2, :], 0.0).then_inc(zero, 1)
            eng.wait_ge(zero, 4)

            def body(b, it, l, A, Bh, F, first):
                def copy(dst, src, rows):
                    if isinstance(b, int):
                        return eng.tensor_tensor(dst, src, zeros[rows, :, :], ALU.add)
                    return eng.tensor_copy(dst, src)

                if A:
                    if not first:
                        eng.wait_ge(fx, it + (1 - B) + FREE)
                    eng.wait_ge(proj, it * (UNITS + 4) + FREE)
                    eng.wait_ge(radd, it * UNITS + FREE)
                    for rows, off in ((slice(0, 64), 1), (slice(64, P), 0)):
                        copy(sT[rows, :].rearrange("p (a t) -> p a t", a=1), xs[rows, seq(b, 0), off:off + T], rows).then_inc(shifted, 1)
                if F:
                    eng.wait_ge(fxc, it - 2 + FREE)
                    eng.wait_ge(x_d, it - 1 + FREE)
                    for rows, off in ((slice(0, 64), 1), (slice(64, P), 0)):
                        copy(s2[rows, :].rearrange("p (a t) -> p a t", a=1), xs[rows, seq(b, 2), off:off + T], rows).then_inc(fsh, 1)
                if A:
                    eng.wait_ge(shifted, it * 2 + 2)
                    if F:
                        eng.wait_ge(fsh, it * 2 - 2)
                    eng.wait_ge(hat_d, it * PAIRS + FREE)
                    for u in range(UNITS):
                        eng.wait_ge(rotm, it * UNITS + u + 1)
                        eng.tensor_tensor(rot[:, u, :], qc[:, u % 2, :], ps_[:, u % 2, :], ALU.add).then_inc(radd, 1)

            pipeline(eng, body)

        @block.scalar
        def _(eng):
            eng.sem_inc(oev, FREE)
            eng.sem_inc(mr_d, FREE)
            eng.wait_ge(s_const, 16 * 7)
            eng.activation(gates[:, :], xv[:, 4:6], ACT.Tanh).then_inc(gate, 1)
            eng.preload_act_table_set("natural_log_exp_and_others")
            eng.wait_ge(zero, 3)
            with eng.Fori(0, B) as b:
                eng.wait_ge(xst, b + 1)
                eng.activation(tv[:, 1, :], tv[:, 0, :], ACT.Ln).then_inc(xln, 1)
                eng.wait_ge(xln, b * 2 + 1)
                eng.activation(tv[:, 2, :], tv[:, 1, :], ACT.Exp, scale=-0.5).then_inc(xln, 1)
                eng.wait_ge(xtr, b * 6 + 2 + FREE)
                eng.activation(x1[:, bass.ds(b, 1), :].rearrange("p a t -> p (a t)"), ps[:, 0, 0:T], ACT.Copy).then_inc(xev, 1)
                eng.wait_ge(xtr, b * 6 + 4 + FREE)
                eng.activation(cT, ps[:, 1, 0:T], ACT.Copy).then_inc(xev, 1)
                eng.wait_ge(xtr, b * 6 + 6 + FREE)
                eng.activation(xhT, ps[:, 2, 0:T], ACT.Copy).then_inc(xev, 1)
                eng.wait_ge(xqk, b * 2 + 2)
                eng.activation(kTb, kT, ACT.Copy).then_inc(xpadb, 1)
                for i in range(4):
                    eng.wait_ge(xpad, b * H + 4 * i + 4)
                    eng.activation(qpadb[:, 4 * i:4 * i + 4, :], qpad[:, 4 * i:4 * i + 4, :], ACT.Copy).then_inc(xpadb, 1)
                eng.wait_ge(xmt, b + 1)
                eng.activation(mrow[:, 0:T], ps[0:H, 0, 0:T], ACT.Copy).then_inc(xmr, 1)
                for n in range(2 * PAIRS):
                    pr, kt = divmod(n, 2)
                    eng.wait_ge(xsc, b * 2 * PAIRS + n + 1)
                    if n >= 4:
                        eng.wait_ge(xav, b * PAIRS + (n - 4) // 2 + 1)
                    eng.activation(xP[:, n % 4, :, :], ps[:, 2 + n % 4, :].rearrange("p (a t) -> p a t", a=2),
                                   ACT.Exp).then_inc(xex, 1)

            for c in range(CH):
                eng.wait_ge(nxc, c + 1)
                eng.activation(sq0[:, c, :], xc0[:, c, :], ACT.Square).then_inc(nsq, 1)
            for c in range(CH):
                eng.wait_ge(nva, c + 1)
                eng.activation(z0[:, c, :], va0[:, c, :], ACT.Ln).then_inc(nln, 1)
            for c in range(CH):
                eng.wait_ge(nln, c + 1)
                eng.activation(z0[:, c, :], z0[:, c, :], ACT.Exp, scale=-0.5).then_inc(ny, 1)

            def body(b, it, l, A, Bh, F, first):
                def evict_v(j):
                    n, c = j % 2, j // 2
                    eng.wait_ge(proj, it * (UNITS + 4) + (UNITS + j + 1 + FREE))
                    if Bh:
                        eng.wait_ge(ov_d, it * PAIRS + (4 * c + 4 - PAIRS))
                    eng.activation(vs[:, n, c * 512:c * 512 + 512], ps[:, j % 2, :], ACT.Copy).then_inc(vev, 1)

                def evict_o(p):
                    eng.wait_ge(ov_d, it * PAIRS + (p + 1 - PAIRS))
                    eng.activation(osb[:, p, :], ps[:, 7, 0:T], ACT.Copy).then_inc(oev, 1)

                for s in range(PAIRS):
                    for kind, i in steps[s]:
                        if kind == "u" and A:
                            eng.wait_ge(proj, it * (UNITS + 4) + (i + 1 + FREE))
                            if i >= 8:
                                eng.wait_ge(sums, it * UNITS + (i - 7 + FREE))
                            eng.activation(sq[:, i % 8, :], ps[:, i % 2, 0:T], ACT.Square).then_inc(sq_d, 1)
                        if kind == "h" and Bh:
                            eng.wait_ge(st_d, it * H + (i + 1 - H))
                            if i >= 4:
                                eng.wait_ge(ov_d, it * PAIRS + ((i - 4) // 2 + 1 - PAIRS))
                            eng.activation(pt[:, i % 4, :], ps[:, 5 + i % 2, 0:QW + P], ACT.Exp).then_inc(ex_d, 1)
                        if kind == "v" and A:
                            evict_v(i)
                    if Bh and s:
                        evict_o(s - 1)
                    if F and s == 1:
                        eng.wait_ge(fxc, it - 1 + FREE)
                        eng.activation(sq2, xc, ACT.Square).then_inc(fsq, 1)
                    if F and s == 2:
                        eng.wait_ge(fva, it - 1)
                        eng.activation(y1, va, ACT.Ln).then_inc(fln, 1)
                        eng.wait_ge(fln, it - 1)
                        eng.activation(y0, y1, ACT.Exp, scale=-0.5).then_inc(fy, 1)
                    if F and s == 5:
                        eng.wait_ge(fev, it * 4 - 4)
                        eng.activation(gel, gt, ACT.Gelu).then_inc(fg, 1)
                        eng.preload_act_table_set("natural_log_exp_and_others")
                    if A and s == PAIRS - 1:
                        eng.wait_ge(ss_d, it + 1)
                        eng.activation(n_t, n_s, ACT.Ln, scale=65536.0).then_inc(ln_d, 1)
                        eng.wait_ge(ln_d, it + 1)
                        eng.activation(n_y, n_t, ACT.Exp, scale=-0.5).then_inc(y_d, 1)
                if Bh:
                    evict_o(PAIRS - 1)
                if A:
                    evict_v(2)
                    evict_v(3)
                if Bh:
                    eng.wait_ge(dev, it)
                    eng.activation(d_t, d_s, ACT.Ln).then_inc(dln, 1)
                    eng.wait_ge(dln, it)
                    eng.activation(d_y, d_t, ACT.Exp, scale=-1.0).then_inc(dy, 1)
                if A:
                    for n, i in enumerate(HATS):
                        eng.wait_ge(hat_d, it * PAIRS + (n + 1 + FREE))
                        eng.activation(hatb[:, 2 * i:2 * i + 2, :], hat[:, 2 * i:2 * i + 2, :], ACT.Copy).then_inc(hatb_d, 1)
                    eng.wait_ge(mt_d, it + 1)
                    eng.activation(mrow[:, 0:QW], ps[0:H, 2, 0:QW], ACT.Copy).then_inc(mr_d, 1)
                    eng.activation(mrow[:, QW:QW + P], ps[0:H, 2, P:T], ACT.Copy).then_inc(mr_d, 1)

            pipeline(eng, body)
            for b in range(B):
                eng.wait_ge(tr_o, b + 1)
                if b >= 2:
                    eng.wait_ge(s_out[b % 2], 16 * (b // 2))
                eng.activation(otok[:, b % 2, :, :], ps[:, b % 2, 0:T].rearrange("p (n d) -> p n d", n=NT),
                               ACT.Copy).then_inc(ev_o, 1)

        @block.vector
        def _(eng):
            for s in (hat_d, xres, on_d, fx, fxc, x_d):
                eng.sem_inc(s, FREE)
            eng.wait_ge(s_const, 16 * 7)
            eng.wait_ge(zero, 3)
            with eng.Fori(0, B) as b:
                eng.wait_ge(s_x, b * 32 + 32)
                for n in range(NT):
                    eng.bn_stats(bst[:, n, :], xtok[:, n, :]).then_inc(chain, 1)
                PER = 13
                base = lambda c: b * PER + c
                eng.wait_ge(chain, base(2))
                eng.tensor_tensor(tv[:, 1, :], bst[:, :, 1], bst[:, :, 4], ALU.subtract).then_inc(chain, 1)
                eng.tensor_tensor(tv[:, 2, :], bst[:, :, 2], bst[:, :, 5], ALU.add).then_inc(chain, 1)
                eng.tensor_tensor(bag[:, 1, :], bst[:, :, 1], bst[:, :, 4], ALU.add).then_inc(chain, 1)
                eng.wait_ge(chain, base(5))
                eng.scalar_tensor_tensor(tv[:, 1, :], tv[:, 1, :], 0.25, tv[:, 1, :], ALU.mult, ALU.mult).then_inc(chain, 1)
                eng.tensor_scalar(tv[:, 2, :], tv[:, 2, :], 1.0 / P, EPS, ALU.mult, ALU.add).then_inc(chain, 1)
                eng.tensor_scalar(bag[:, 0, :], bag[:, 1, :], 0.5, None, ALU.mult).then_inc(chain, 1)
                eng.wait_ge(chain, base(8))
                eng.tensor_tensor(tv[:, 0, :], tv[:, 1, :], tv[:, 2, :], ALU.add).then_inc(xst, 1)
                eng.wait_ge(xln, b * 2 + 2)
                eng.tensor_tensor(tv[:, 3, :], tv[:, 2, :], tv[:, 2, :], ALU.mult).then_inc(chain, 1)
                eng.wait_ge(chain, base(9))
                eng.scalar_tensor_tensor(tv[:, 3, :], tv[:, 3, :], -0.5, tv[:, 0, :], ALU.mult, ALU.mult).then_inc(chain, 1)
                eng.wait_ge(chain, base(10))
                eng.scalar_tensor_tensor(tv[:, 4, :], tv[:, 3, :], 1.5, tv[:, 2, :], ALU.add, ALU.mult).then_inc(chain, 1)
                eng.wait_ge(chain, base(11))
                for n in range(NT):
                    eng.tensor_scalar(xhat[:, n, :], xtok[:, n, :], bag[:, 0, n:n + 1], tv[:, 4, n:n + 1],
                                      ALU.subtract, ALU.mult).then_inc(xhat_d, 1)
                eng.wait_ge(xpr, b * 4 + 1)
                eng.tensor_scalar(qT, ps[:, 3, 0:T], xv_q, float(np.float32(1) / np.sqrt(np.float32(XD))),
                                  ALU.add, ALU.mult).then_inc(xqk, 1)
                eng.wait_ge(xpr, b * 4 + 2)
                eng.tensor_scalar(kT, ps[:, 4, 0:T], xv_k, None, ALU.add).then_inc(xqk, 1)
                eng.wait_ge(xqk, b * 2 + 1)
                for i in range(H):
                    eng.tensor_scalar(qpad[:, i, :], qT, hmask[:, hd[i]:hd[i] + 1], None, ALU.mult).then_inc(xpad, 1)
                eng.wait_ge(xpr, b * 4 + 4)
                vsrc = ps[:, 5, 0:T].rearrange("p (n a j d) -> p n a j d", n=NT, a=4, j=4)
                vdst = vpad.rearrange("p n (a j) (m d) -> p n a j m d", j=4, m=4)
                for n in range(NT):
                    for j in range(4):
                        eng.tensor_copy(vdst[:, n, :, j, j, :], vsrc[:, n, :, j, :]).then_inc(xvp, 1)
                for n in range(NT * PAIRS):
                    t_, pr = divmod(n, PAIRS)
                    eng.wait_ge(xs_d, b * NT * PAIRS + n + 1)
                    eng.tensor_reduce(mcol[:, t_, 2 * pr:2 * pr + 2], ps[:, 6 + n % 2, :].rearrange("p (a t) -> p a t", a=2),
                                      AX.X, ALU.max, negate=True).then_inc(xmax, 1)
                eng.wait_ge(xav, b * PAIRS + PAIRS)
                eng.reciprocal(xrd, ps[:, 7, 0:T]).then_inc(xrd_d, 1)
                eng.wait_ge(xrd_d, b + 1)
                eng.tensor_tensor(xo, ps[:, 6, 0:T], xrd, ALU.mult).then_inc(chain, 1)
                eng.wait_ge(chain, base(12))
                eng.tensor_scalar(xo2, xo, xv_v, None, ALU.add).then_inc(xo_d, 1)
                eng.wait_ge(xwo, b + 1)
                eng.wait_ge(gate, 1)
                eng.tensor_scalar(xproj, ps[:, 0, 0:T], xv_o, gates[:, 0:1], ALU.add, ALU.mult).then_inc(chain, 1)
                eng.wait_ge(chain, base(13))
                x1b = x1[:, bass.ds(b, 1), :].rearrange("p a t -> p (a t)")
                eng.tensor_tensor(x1b, x1b, xproj, ALU.add).then_inc(xres, 1)

            for c in range(CH):
                eng.wait_ge(nmean, c + 1)
                eng.tensor_tensor(xc0[:, c, :], x1[:, 2 * c:2 * c + 2, :].rearrange("p a t -> p (a t)"), ps[:, c, :],
                                  ALU.subtract).then_inc(nxc, 1)
            for c in range(CH):
                eng.wait_ge(nvar, c + 1)
                eng.tensor_scalar(va0[:, c, :], ps[:, 4 + c, :], EPS, None, ALU.add).then_inc(nva, 1)
            for c in range(CH):
                eng.wait_ge(ny, c + 1)
                eng.tensor_tensor(z1[:, c, :], z0[:, c, :], z0[:, c, :], ALU.mult).then_inc(nt, 1)
            for c in range(CH):
                eng.wait_ge(nt, c + 1)
                eng.scalar_tensor_tensor(z1[:, c, :], z1[:, c, :], -0.5, va0[:, c, :], ALU.mult, ALU.mult).then_inc(nt, 1)
            for c in range(CH):
                eng.wait_ge(nt, CH + c + 1)
                eng.scalar_tensor_tensor(z1[:, c, :], z1[:, c, :], 1.5, z0[:, c, :], ALU.add, ALU.mult).then_inc(nt, 1)
            for c in range(CH):
                eng.wait_ge(nt, 2 * CH + c + 1)
                eng.tensor_tensor(xs[:, 2 * c:2 * c + 2, 1:T + 1], xc0[:, c, :].rearrange("p (a t) -> p a t", a=2),
                                  z1[:, c, :].rearrange("p (a t) -> p a t", a=2), ALU.mult).then_inc(nxn, 1)

            def layer_start(l, first):
                src = vecs[:, 0, 0:4] if first else vecs[:, bass.ds(l, 1), 0:4].rearrange("p a n -> p (a n)")
                eng.tensor_copy(va_c[:, :], src).then_inc(vcur, 1)
                eng.wait_ge(vcur, l + 1)
                for i in range(4):
                    eng.tensor_scalar(tab[:, i, :], rot_base[:, i, :], va_c[:, i:i + 1], None, ALU.mult).then_inc(tabs, 1)

            def layer_second(l, first):
                src = vecs[:, 0, :] if first else vecs[:, bass.ds(l, 1), :].rearrange("p a n -> p (a n)")
                eng.tensor_copy(vf[:, :], src).then_inc(fvc, 1)

            def body(b, it, l, A, Bh, F, first):
                def norm_ffn():
                    fb = lambda c: it * 4 + (c - 8)
                    eng.wait_ge(fy, it - 1)
                    eng.tensor_tensor(y1, y0, y0, ALU.mult).then_inc(fchain, 1)
                    eng.wait_ge(fchain, fb(1))
                    eng.scalar_tensor_tensor(y1, y1, -0.5, va, ALU.mult, ALU.mult).then_inc(fchain, 1)
                    eng.wait_ge(fchain, fb(2))
                    eng.scalar_tensor_tensor(y1, y1, 1.5, y0, ALU.add, ALU.mult).then_inc(fchain, 1)
                    eng.wait_ge(fchain, fb(3))
                    eng.tensor_tensor(xc, xc, y1, ALU.mult).then_inc(fchain, 1)
                    eng.wait_ge(fchain, fb(4))
                    eng.tensor_scalar(xn, xc, vf[:, 4:5], vf[:, 5:6], ALU.mult, ALU.add).then_inc(fxn, 1)

                def ffn(s):
                    f3, f4 = it * 3 - 6, it * 4 - 8
                    if s == 1:
                        eng.wait_ge(fmean, it - 1)
                        eng.wait_ge(fsh, it * 2 - 2)
                        eng.tensor_tensor(xc, s2, ps[:, 3, 0:T], ALU.subtract).then_inc(fxc, 1)
                    if s == 2:
                        eng.wait_ge(fvar, it - 1)
                        eng.tensor_scalar(va, ps[:, 3, 0:T], EPS, None, ALU.add).then_inc(fva, 1)
                    if s == 3:
                        norm_ffn()
                    if s == 4:
                        eng.wait_ge(fh, f3 + 1)
                        for j in range(2):
                            eng.tensor_scalar(gt[:, j, :], ps[:, 3, j * T:j * T + T], vf[:, 9 + j:10 + j], None,
                                              ALU.add).then_inc(fev, 1)
                    if s == 5:
                        m = HC[2][1]
                        eng.wait_ge(fh, f3 + 2)
                        eng.tensor_scalar(gt[0:m, 2, :], ps[0:m, 3, 0:T], vf[0:m, 11:12], None, ALU.add).then_inc(fev, 1)
                        eng.tensor_scalar(a2[0:m, :], ps[0:m, 3, T:2 * T], vf[0:m, 8:9], None, ALU.add).then_inc(fev, 1)
                    if s == 6:
                        m = HC[2][1]
                        eng.wait_ge(fh, f3 + 3)
                        eng.wait_ge(fg, it - 1)
                        for j in range(2):
                            eng.scalar_tensor_tensor(uu[:, j, :], ps[:, 3, j * T:j * T + T], vf[:, 6 + j:7 + j],
                                                     gel[:, j, :], ALU.add, ALU.mult).then_inc(fu, 1)
                        eng.tensor_tensor(uu[0:m, 2, :], a2[0:m, :], gel[0:m, 2, :], ALU.mult).then_inc(fu, 1)
                    if s == 7:
                        eng.wait_ge(fo, it - 1 + FREE)
                        xb = xs[:, seq(b, 2), 1:T + 1]
                        eng.scalar_tensor_tensor(xb, ps[:, 3:4, 0:T], vf[:, 12:13], xb, ALU.add, ALU.add).then_inc(fx, 1)

                if A:
                    eng.wait_ge(tabs, l * 4 + 4)
                if F:
                    eng.wait_ge(fvc, l if isinstance(b, int) else l + 1)
                for s in range(PAIRS):
                    for kind, u in steps[s]:
                        if kind == "u" and A:
                            k = u // PAIRS
                            eng.wait_ge(sq_d, it * UNITS + (u + 1))
                            if u >= 2:
                                eng.wait_ge(radd, it * UNITS + (u - 1 + FREE))
                            eng.tensor_tensor(qc[:, u % 2, :], ps[:, u % 2, 0:T], tab[:, 2 * k, :], ALU.mult)
                            eng.tensor_tensor(ps_[:, u % 2, :], ps[:, u % 2, T:2 * T], tab[:, 2 * k + 1, :],
                                              ALU.mult).then_inc(rotm, 1)
                    if A and s == PAIRS - 1:
                        eng.wait_ge(sums, it * UNITS + (UNITS + FREE))
                        eng.tensor_scalar(n_s, ps[:, 2, 0:T], 1e-24, None, ALU.max).then_inc(ss_d, 1)
                    if F:
                        ffn(s)
                if A:
                    eng.wait_ge(y_d, it + 1)
                    nb = lambda c: it * 6 + c
                    eng.tensor_scalar(n_y, n_y, 256.0, None, ALU.mult).then_inc(nchain, 1)
                    eng.wait_ge(nchain, nb(1))
                    eng.tensor_tensor(n_t, n_y, n_y, ALU.mult).then_inc(nchain, 1)
                    eng.wait_ge(nchain, nb(2))
                    eng.scalar_tensor_tensor(n_t, n_t, -0.5, n_s, ALU.mult, ALU.mult).then_inc(nchain, 1)
                    eng.wait_ge(nchain, nb(3))
                    eng.scalar_tensor_tensor(n_r, n_t, 1.5, n_y, ALU.add, ALU.mult).then_inc(nchain, 1)
                    eng.wait_ge(nchain, nb(4))
                    eng.tensor_copy(n_hi, n_r).then_inc(nchain, 1)
                    eng.wait_ge(nchain, nb(5))
                    eng.scalar_tensor_tensor(n_z, n_hi, part["parts"][:, 0:1], n_r, ALU.mult, ALU.add).then_inc(nchain, 1)
                    eng.wait_ge(nchain, nb(6))
                    eng.tensor_copy(n_mid, n_z).then_inc(nmid, 1)
                    eng.wait_ge(nmid, it + 1)
                    eng.scalar_tensor_tensor(n_parts, n_mid, part["parts"][:, 1:2], n_z, ALU.mult, ALU.add).then_inc(r_d, 1)
                if Bh:
                    eng.wait_ge(ov_d, it * PAIRS)
                    eng.tensor_copy(d_s, ps[:, 4, 0:T]).then_inc(dev, 1)

                def make_hat(n):
                    i = HATS[n]
                    eng.wait_ge(rb, it * PAIRS + (n + 1))
                    eng.wait_ge(radd, it * UNITS + (2 * i + 2 + FREE))
                    if Bh and n == 0:
                        eng.wait_ge(st_d, it * H)
                    eng.tensor_tensor(hat[:, 2 * i:2 * i + 2, :], rot[:, 2 * i:2 * i + 2, :],
                                      ps[:, n % 2, :].rearrange("p (a t) -> p a t", a=2), ALU.mult).then_inc(hat_d, 1)

                for g in range(5):
                    if A and g < 4:
                        make_hat(2 * g)
                        make_hat(2 * g + 1)
                    if Bh and g == 0:
                        db = lambda c: it * 5 + (c - 5)
                        eng.wait_ge(dy, it)
                        eng.tensor_tensor(d_t, d_s, d_y, ALU.mult).then_inc(dchain, 1)
                        eng.wait_ge(dchain, db(1))
                        eng.scalar_tensor_tensor(d_r, d_t, -2.0, d_y, ALU.add, ALU.mult).then_inc(dchain, 1)
                        eng.wait_ge(dchain, db(2))
                        eng.tensor_copy(d_hi, d_r).then_inc(dchain, 1)
                        eng.wait_ge(dchain, db(3))
                        eng.scalar_tensor_tensor(d_z, d_hi, part["parts"][:, 2:3], d_r, ALU.mult, ALU.add).then_inc(dchain, 1)
                        eng.wait_ge(dchain, db(4))
                        eng.tensor_copy(d_mid, d_z).then_inc(dchain, 1)
                        eng.wait_ge(dchain, db(5))
                        eng.scalar_tensor_tensor(d_parts, d_mid, part["parts"][:, 3:4], d_z, ALU.mult, ALU.add).then_inc(dp, 1)
                    if A and g:
                        for h in range(4 * g - 4, 4 * g):
                            eng.wait_ge(sc_d, it * H + (h + 1))
                            eng.tensor_reduce(mcol[:, :, h:h + 1].rearrange("p a b -> p (a b)"),
                                              ps[:, 3 + h % 2, 0:2 * QW].rearrange("p (a t) -> p a t", a=2), AX.X, ALU.max,
                                              negate=True).then_inc(max_d, 1)
                    if Bh and g:
                        i = g - 1
                        eng.wait_ge(rdb, it * 4 + (i + 1 - 4))
                        eng.wait_ge(oev, it * PAIRS + (2 * i + 2 - PAIRS + FREE))
                        eng.tensor_tensor(osb[:, 2 * i:2 * i + 2, :], osb[:, 2 * i:2 * i + 2, :],
                                          ps[:, 5 + i % 2, :].rearrange("p (a t) -> p a t", a=2), ALU.mult).then_inc(on_d, 1)
                if Bh:
                    eng.wait_ge(wo_d, it + FREE)
                    xb = xs[:, seq(b, 1), 1:T + 1]
                    eng.tensor_tensor(xb, xb, ps[:, 7:8, 0:T], ALU.add).then_inc(x_d, 1)

            pipeline(eng, body, layer_start, layer_second)
            eng.wait_ge(fx, L * B + FREE)
            for b in range(B):
                eng.scalar_tensor_tensor(x1[:, b, :], xs[:, b, 1:T + 1], gates[:, 1:2], x1[:, b, :], ALU.mult,
                                         ALU.add).then_inc(gx, 1)

        @block.tensor
        def _(eng):
            for s in (xtr, proj, sums, wo_d, fo):
                eng.sem_inc(s, FREE)
            eng.wait_ge(s_const, 16 * 7)
            eng.wait_ge(cast, CASTS)
            with eng.Fori(0, B) as b:
                eng.wait_ge(s_x, b * 32 + 32)
                eng.wait_ge(xres, b + FREE)
                for n in range(NT):
                    eng.transpose(ps[:, 0, n * P:n * P + P], xtok[:, n, :], ident).then_inc(xtr, 1)
                for n in range(NT):
                    eng.transpose(ps[:, 1, n * P:n * P + P], ctok[:, n, :], ident).then_inc(xtr, 1)
                for n in range(NT):
                    eng.wait_ge(xhat_d, b * NT + n + 1)
                    eng.transpose(ps[:, 2, n * P:n * P + P], xhat[:, n, :], ident).then_inc(xtr, 1)
                eng.wait_ge(xev, b * 3 + 3)
                eng.matmul(ps[:, 3, 0:T], xw_sb[:, 0, :], xhT, start=True, stop=True).then_inc(xpr, 1)
                eng.matmul(ps[:, 4, 0:T], xw_sb[:, 1, :], cT, start=True, stop=True).then_inc(xpr, 1)
                for n in range(NT):
                    eng.matmul(ps[:, 5, n * P:n * P + P], cT[:, n * P:n * P + P], xw_sb[:, 2, :],
                               start=True, stop=True).then_inc(xpr, 1)
                eng.wait_ge(xpadb, b * 5 + 5)
                for n in range(NT * PAIRS):
                    t_, pr = divmod(n, PAIRS)
                    if n >= 2:
                        eng.wait_ge(xmax, b * NT * PAIRS + n - 1)
                    for a in range(2):
                        mm = eng.matmul(ps[:, 6 + n % 2, a * T:a * T + T], qpadb[:, 2 * pr + a, t_ * P:t_ * P + P], kTb,
                                        start=True, stop=True)
                    mm.then_inc(xs_d, 1)
                eng.wait_ge(xmax, b * NT * PAIRS + NT * PAIRS)
                for n in range(NT):
                    mm = eng.transpose(ps[0:H, 0, n * P:n * P + P], mcol[:, n, :], ident)
                mm.then_inc(xmt, 1)
                eng.wait_ge(xvp, b * 8 + 8)

                def score(n):
                    pr, kt = divmod(n, 2)
                    if n >= 4:
                        eng.wait_ge(xex, b * 2 * PAIRS + n - 3)
                    bank = ps[:, 2 + n % 4, :]
                    eng.matmul(bank, kT[:, kt * P:kt * P + P], qpad[:, 2 * pr:2 * pr + 2, :].rearrange("p a t -> p (a t)"),
                               start=True, stop=False, skip_group_check=True)
                    if n == 0:
                        eng.wait_ge(xmr, b + 1)
                    for a in range(2):
                        mm = eng.matmul(bank[:, a * T:a * T + T], onehot[:, 2 * pr + a, :], mrow[:, 0:T],
                                        start=False, stop=a == 1, skip_group_check=True)
                    mm.then_inc(xsc, 1)

                def weigh(pr):
                    eng.wait_ge(xex, b * 2 * PAIRS + 2 * pr + 2)
                    for kt in range(NT):
                        for bank in (6, 7):
                            for a in range(2):
                                h = hd[2 * pr + a]
                                g = h // 4
                                w = vpad[:, kt, h, :] if bank == 6 else xones[:, h % 4, :]
                                first = h % 4 == 0 and kt == 0
                                mm = eng.matmul(ps[32 * g:32 * g + 32, bank, 0:T], w, xP[:, (2 * pr + kt) % 4, a, :],
                                                start=first, stop=h % 4 == 3 and kt == 1, skip_group_check=True)
                    mm.then_inc(xav, 1)

                for pr in range(PAIRS):
                    score(2 * pr)
                    score(2 * pr + 1)
                    if pr:
                        weigh(pr - 1)
                weigh(PAIRS - 1)
                eng.wait_ge(xo_d, b + 1)
                eng.matmul(ps[:, 0, 0:T], xw_sb[:, 3, :], xo2, start=True, stop=True).then_inc(xwo, 1)

            eng.wait_ge(xres, B + FREE)
            for c in range(CH):
                eng.matmul(ps[:, c, :], mean_w, x1[:, 2 * c:2 * c + 2, :].rearrange("p a t -> p (a t)"),
                           start=True, stop=True).then_inc(nmean, 1)
            for c in range(CH):
                eng.wait_ge(nsq, c + 1)
                eng.matmul(ps[:, 4 + c, :], mean_w, sq0[:, c, :], start=True, stop=True).then_inc(nvar, 1)
            eng.wait_ge(nxn, CH)


            def body(b, it, l, A, Bh, F, first):
                if A:
                    eng.wait_ge(shifted, it * 2 + 2)
                    if isinstance(b, int) and b == 0:
                        eng.wait_ge(s_w, l * 32 + 32)
                    eng.wait_ge(hat_d, it * PAIRS + FREE)

                def project(u):
                    if u >= 2:
                        eng.wait_ge(rotm, it * UNITS + (u - 1))
                        eng.wait_ge(sq_d, it * UNITS + (u - 1))
                    eng.matmul(ps[:, u % 2, 0:T], wn_sb[:, u * P:u * P + P], sT, start=True, stop=True)
                    eng.matmul(ps[:, u % 2, T:2 * T], wp_sb[:, u * P:u * P + P], sT, start=True, stop=True).then_inc(proj, 1)

                def head_sums(g):
                    for u in range(4 * g, 4 * g + 4):
                        eng.wait_ge(sq_d, it * UNITS + (u + 1))
                        if u == 0:
                            eng.wait_ge(mr_d, it * 2 + FREE)
                        q = u % 4
                        eng.matmul(ps[32 * q:32 * q + 32, 2, 0:T], sumsel[:, g, :], sq[:, u % 8, :],
                                   start=g == 0, stop=g == 3, skip_group_check=True).then_inc(sums, 1)

                def values(j):
                    n, c = j % 2, j // 2
                    if j < 2:
                        eng.wait_ge(rotm, it * UNITS + (UNITS - 1 + j))
                    else:
                        eng.wait_ge(vev, it * 4 + (j - 1))
                    eng.matmul(ps[:, j % 2, :], sT[:, n * P:n * P + P], wn_sb[:, 2 * INNER + c * 512:2 * INNER + c * 512 + 512],
                               start=True, stop=True).then_inc(proj, 1)

                def score(h):
                    p, r = divmod(h, 2)
                    rows = slice(64 * r, 64 * r + 64)
                    if h >= 2:
                        eng.wait_ge(ex_d, it * H + (h - 1 - H))
                    bank = ps[:, 5 + r, :]
                    eng.matmul(bank[:, 0:QW + P], ident_b[:, :], mask_tb[:, :], start=True, stop=False, skip_group_check=True)
                    if h == 0:
                        eng.wait_ge(mr_d, it * 2 + FREE)
                    eng.matmul(bank[:, 0:QW + P], onehot[:, h, :], mrow[:, :], start=False, stop=False, skip_group_check=True)
                    for n, (lo, w) in enumerate(((0, QW), (QW, P))):
                        mm = eng.matmul(bank[:, lo:lo + w], hat[rows, PAIRS + p, n * P:n * P + P], hat[rows, p, n * P:n * P + w],
                                        start=False, stop=n == 1, skip_group_check=True)
                    mm.then_inc(st_d, 1)

                def weigh(p):
                    eng.wait_ge(ex_d, it * H + (2 * p + 2 - H))
                    if p:
                        eng.wait_ge(oev, it * PAIRS + (p - PAIRS + FREE))
                    else:
                        eng.wait_ge(x_d, it - 1 + FREE)
                    for n, (lo, w) in enumerate(((0, QW), (QW, P))):
                        for r in range(2):
                            h = 2 * p + r
                            mm = eng.matmul(ps[64 * r:64 * r + 64, 7, n * P:n * P + w],
                                            vs[:, n, h * D:h * D + D], pt[:, h % 4, lo:lo + w],
                                            start=n == 0, stop=n == 1, skip_group_check=True)
                    for n, (lo, w) in enumerate(((0, QW), (QW, P))):
                        for r in range(2):
                            h = 2 * p + r
                            g = h % 4
                            mm = eng.matmul(ps[32 * g:32 * g + 32, 4, n * P:n * P + w], densel[:, h // 4, :],
                                            pt[:, h % 4, lo:lo + w], start=h < 4 and n == 0,
                                            stop=h >= 12 and n == 1, skip_group_check=True)
                    mm.then_inc(ov_d, 1)

                def ffn(s):
                    f4 = it * 4 - 8
                    def up(col, j, at, stop=True):
                        o, m = HC[j]
                        o += HID * (col == "gate")
                        return eng.matmul(ps[0:m, 3, at:at + T], w1_sb[:, o:o + m], xn, start=True, stop=True)
                    if s == 1:
                        eng.wait_ge(fsh, it * 2 - 2)
                        eng.matmul(ps[:, 3, 0:T], mean_w, s2, start=True, stop=True).then_inc(fmean, 1)
                    if s == 2:
                        eng.wait_ge(fsq, it - 1)
                        eng.matmul(ps[:, 3, 0:T], mean_w, sq2, start=True, stop=True).then_inc(fvar, 1)
                    if s == 4:
                        if not isinstance(b, int):
                            eng.wait_ge(s_wf, l * 32 + 32)
                        eng.wait_ge(fxn, it - 1)
                        up("gate", 0, 0)
                        up("gate", 1, T).then_inc(fh, 1)
                    if s == 5:
                        eng.wait_ge(fev, f4 + 2)
                        up("gate", 2, 0)
                        up("a", 2, T).then_inc(fh, 1)
                    if s == 6:
                        eng.wait_ge(fev, f4 + 4)
                        up("a", 0, 0)
                        up("a", 1, T).then_inc(fh, 1)
                    if s == 7:
                        for j, (_, m) in enumerate(HC):
                            eng.wait_ge(fu, it * 3 + (3 - 6))
                            mm = eng.matmul(ps[:, 3, 0:T], w2_sb[0:m, j, :], uu[0:m, j, :], start=j == 0, stop=j == 2)
                        mm.then_inc(fo, 1)

                group = 0
                for s in range(PAIRS):
                    for kind, i in steps[s]:
                        if kind == "u" and A:
                            project(i)
                        if kind == "h" and Bh:
                            score(i)
                        if kind == "v" and A:
                            values(i)
                        if A and s == PAIRS - 1 and group < 4:
                            head_sums(group)
                            group += 1
                    if F:
                        ffn(s)
                    if Bh and s:
                        weigh(s - 1)
                    if A and group < 4 and 4 * group + 4 <= first_unit[s]:
                        head_sums(group)
                        group += 1
                if Bh:
                    weigh(PAIRS - 1)
                if A:
                    values(2)
                    values(3)

                def spread(n):
                    if n < 2:
                        eng.wait_ge(vev, it * 4 + (3 + n))
                    else:
                        eng.wait_ge(hat_d, it * PAIRS + (n - 1 + FREE))
                    for a in range(2):
                        mm = eng.matmul(ps[:, n % 2, a * T:a * T + T], rselb[:, 2 * HATS[n] + a, :], n_parts, start=True, stop=True)
                    mm.then_inc(rb, 1)

                def row_score(h):
                    p, r = divmod(h, 2)
                    rows = slice(64 * r, 64 * r + 64)
                    if r == 0:
                        eng.wait_ge(hatb_d, it * PAIRS + (2 * (p // 2) + 2))
                    if h >= 2:
                        eng.wait_ge(max_d, it * H + (h - 1))
                    elif h == 0 and F:
                        eng.wait_ge(fx, it - 1 + FREE)
                    elif h == 1 and Bh:
                        eng.wait_ge(dev, it)
                    bank = ps[:, 3 + r, :]
                    eng.matmul(bank[:, 0:2 * QW], ident_b[:, :], mask_sb[:, :], start=True, stop=False, skip_group_check=True)
                    eng.matmul(bank[:, WIN:QW], hatb[rows, p, 0:P], hatb[rows, PAIRS + p, 0:P], start=False, stop=False,
                               skip_group_check=True)
                    eng.matmul(bank[:, QW:2 * QW], hatb[rows, p, P:T], hatb[rows, PAIRS + p, P - WIN:T],
                               start=False, stop=True, skip_group_check=True).then_inc(sc_d, 1)

                def project_out(p):
                    eng.wait_ge(on_d, it * 4 + (p // 2 + 1 - 4 + FREE))
                    return eng.matmul(ps[:, 7, 0:T], wo_sb[:, p, :], osb[:, p, :], start=p == 0, stop=p == PAIRS - 1)

                if A:
                    eng.wait_ge(r_d, it + 1)
                for g in range(5):
                    if A and g < 4:
                        spread(2 * g)
                        spread(2 * g + 1)
                    if A and g:
                        for h in range(4 * g - 4, 4 * g):
                            row_score(h)
                    if Bh and g:
                        i = g - 1
                        if i == 0:
                            eng.wait_ge(dp, it)
                        if i >= 2:
                            eng.wait_ge(on_d, it * 4 + (i - 1 - 4 + FREE))
                        for a in range(2):
                            mm = eng.matmul(ps[:, 5 + i % 2, a * T:a * T + T], rdselb[:, 2 * i + a, :], d_parts, start=True, stop=True)
                        mm.then_inc(rdb, 1)
                if Bh:
                    if isinstance(b, int) and b == 1:
                        eng.wait_ge(s_wo, l * 16 + 16)
                    for p in range(6):
                        project_out(p)
                if A:
                    eng.wait_ge(max_d, it * H + H)
                    for n in range(NT):
                        mm = eng.transpose(ps[0:H, 2, n * P:n * P + P], mcol[:, n, :], ident)
                    mm.then_inc(mt_d, 1)
                if Bh:
                    project_out(6)
                    project_out(7).then_inc(wo_d, 1)

            pipeline(eng, body)
            for b in range(B):
                eng.wait_ge(gx, b + 1)
                if b >= 2:
                    eng.wait_ge(ev_o, b - 1)
                for n in range(NT):
                    mm = eng.transpose(ps[:, b % 2, n * P:n * P + P], x1[:, b, n * P:n * P + P], ident)
                mm.then_inc(tr_o, 1)


def laid_out(inputs):
    a = {k: np.asarray(v) for k, v in inputs.items()}
    up = "L0_xattn_"
    fp = "L0_ffn_"
    wn = a[fp + "Wqkv"]
    swap = (np.arange(D) + D // 2) % D
    wp = wn[:, :, :2 * INNER].reshape(L, P, 2 * H, D)[..., swap].reshape(L, P, 2 * INNER)
    two = lambda v: np.concatenate([v, v], 1)
    b1 = a[fp + "b1"]
    vec = np.zeros((P, L, NV), np.float32)
    qs, ks = a[fp + "q_scale"], a[fp + "k_scale"]
    for i, v in enumerate([two(qs), two(qs[:, swap]), two(ks), two(ks[:, swap]), a[fp + "ln_g"], a[fp + "ln_b"]]):
        vec[:, :, i] = v.T
    for j, (o, m) in enumerate(HC):
        vec[:m, :, 6 + j] = b1[:, o:o + m].T
        vec[:m, :, 9 + j] = b1[:, HID + o:HID + o + m].T
    vec[:, :, 12] = a[fp + "b2"].T
    w2 = np.zeros((L, P, 3, P), np.float32)
    for j, (o, m) in enumerate(HC):
        w2[:, :m, j, :] = a[fp + "W2"][:, o:o + m, :]
    xw = np.stack([a[up + n].T for n in ("Wq", "Wk", "Wv", "Wo")], 1)
    wide = lambda v: np.broadcast_to(v, (P,))
    xvec = np.stack([a[up + "bq"], a[up + "bk"], a[up + "bv"], a[up + "bo"], wide(a["g_xattn"]), wide(a["g_ffn"])], 1)
    arrays = {
        "x": a["x"].reshape(B * T, P), "ctx": a["ctx_1024"].reshape(B * T, P), "xw": xw, "xvec": xvec,
        "wn": wn, "wp": wp, "wo": a[fp + "Wo"].reshape(L, PAIRS, P, P).transpose(0, 2, 1, 3), "w1": a[fp + "W1"],
        "w2": w2, "vec": vec,
    }
    arrays.update(shape_constants())
    return {k: np.ascontiguousarray(v) for k, v in arrays.items()}


def kernel(**inputs):
    import concourse.bacc as bacc
    from concourse.bass_utils import run_bass_kernel_spmd

    arrays = laid_out(inputs)
    nc = bacc.Bacc("TRN2", target_bir_lowering=False, num_devices=1)
    args = [nc.dram_tensor(f"in_{k}", v.shape, mybir.dt.from_np(v.dtype), kind="ExternalInput").ap()
            for k, v in arrays.items()]
    out = nc.dram_tensor("out_0", (B * T, P), F32, kind="ExternalOutput").ap()
    gated_flamingo(nc, *args, out)
    r = run_bass_kernel_spmd(nc, [{f"in_{k}": v for k, v in arrays.items()}], core_ids=[0])
    return r.results[0]["out_0"].reshape(B, T, P)
```

```python
from contextlib import ExitStack

import numpy as np
import concourse.bass as bass
from concourse import mybir

F32 = mybir.dt.float32
BF16 = mybir.dt.bfloat16
ALU = mybir.AluOpType
ACT = mybir.ActivationFunctionType
AX = mybir.AxisListType

P = 128
B, T = 8, 256
NT = T // P
L = 6
H = 16
XD = P // H
D = 64
INNER = H * D
PAIRS = H // 2
UNITS = 2 * PAIRS
WIN = 32
QW = P + WIN
HID = 341
HC = [(0, 128), (128, 128), (256, 85)]
NV = 13
CH = 4
CW = 512
MASKED = -1.0e30
FREE = 1
EPS = 1e-5
BIG = 30 * 1024


def shape_constants():
    f = np.float32
    half = np.arange(0, D, 2, dtype=f)
    inv_freq = (f(1.0) / (f(10000.0) ** (half / f(D)))).astype(f)
    t = np.arange(T, dtype=f)
    fr = (t[:, None] * inv_freq[None, :]).astype(f)
    base = ((half + f(0.4 * D)) / f(1.4 * D)).astype(f)
    scale = (base[None, :] ** ((t - T // 2) / f(WIN // 2))[:, None]).astype(f)
    cos, sin = np.cos(fr).T, np.sin(fr).T
    scale = scale.T
    sign = np.concatenate([-sin, sin])
    both = lambda a: np.concatenate([a, a])
    cq, sq = both(cos * scale), sign * both(scale)
    ck, sk = both(cos / scale), sign / both(scale)
    rot = np.stack([8.0 * both(cq), 8.0 * both(sq), both(ck), both(sk)], 1).astype(f)
    k, q = np.arange(P)[:, None], np.arange(QW)[None, :]
    seen = ((q // WIN == k // WIN) & (q >= k)) | ((q // WIN == k // WIN + 1) & (q <= k + WIN))
    mask_t = np.where(seen, 0.0, MASKED).astype(f)
    qq, kk = np.arange(P)[:, None], np.arange(QW)[None, :] - WIN
    seen = ((qq // WIN == kk // WIN) & (qq >= kk)) | ((qq // WIN == kk // WIN + 1) & (qq <= kk + WIN))
    mask_s = np.where(seen, 0.0, MASKED).astype(f)
    p = np.arange(P)
    m = p % 32
    sumsel = np.zeros((P, 4, 32), f)
    for j in range(4):
        for c in range(4):
            sumsel[p, j, 8 * c + 2 * j + p // D] = 1
    rsel = np.zeros((P, UNITS, P), f)
    for u in range(UNITS):
        for c in range(3):
            rsel[32 * (u % 4) + 8 * c + 2 * (u // 4) + p // D, u, p] = 256
    parts = -np.stack([(m // 8 >= 1) & (m < 24), m // 8 == 2, (m // 4 >= 1) & (m < 12), m // 4 == 2], 1).astype(f)
    densel = np.zeros((P, 4, 32), f)
    for j in range(4):
        densel[:, j, j::4] = 1
    rdsel = np.zeros((P, PAIRS, P), f)
    for j in range(PAIRS):
        h = 2 * j + p // D
        for c in range(3):
            rdsel[32 * (h % 4) + 4 * c + h // 4, j, p] = -1
    xones = np.zeros((P, 4, 32), f)
    for j in range(4):
        xones[:, j, XD * j:XD * j + XD] = 1
    onehot = np.zeros((H, H, P), f)
    onehot[np.arange(H), np.arange(H), :] = 1
    hmask = np.zeros((P, H), f)
    hmask[p, p // XD] = 1
    flat = lambda a: a.reshape(a.shape[0], -1)
    c128 = np.concatenate([np.eye(P, dtype=f), np.full((P, P), 1.0 / P, f), flat(sumsel), flat(densel),
                           flat(xones), hmask, parts, mask_t, mask_t[:, 0:P],
                           np.full((P, WIN), MASKED, f), mask_s[:, WIN:], mask_s], 1)
    return {"c_rot": flat(rot), "c_sel": np.ascontiguousarray(c128), "c_rsel": np.concatenate([flat(rsel), flat(rdsel)], 1),
            "c_onehot": flat(onehot)}


C_PARTS = [("ident", P), ("mean", P), ("sumsel", 4 * 32), ("densel", 128), ("xones", 128),
           ("hmask", H), ("parts", 4), ("mask_t", QW + P), ("mask_s", 2 * QW)]


def gated_flamingo(nc, x, ctx_in, xw, xvec, wn, wo, w1, w2, vec, c_rot, c_sel, c_rsel, c_onehot, out):
    with ExitStack() as st:
        def sb(name, shape, dt=F32):
            return st.enter_context(nc.sbuf_tensor(name, shape, dt))

        def sem(name):
            return st.enter_context(nc.semaphore(name))

        width = sum(w for _, w in C_PARTS)
        sel = sb("sel", [P, width])
        part, at = {}, 0
        for name, w in C_PARTS:
            part[name] = sel[:, at:at + w]
            at += w
        ident, mean_w, hmask = part["ident"], part["mean"], part["hmask"]
        sumsel = part["sumsel"].rearrange("p (j m) -> p j m", j=4)
        densel = part["densel"].rearrange("p (j m) -> p j m", j=4)
        xones = part["xones"].rearrange("p (j m) -> p j m", j=4)
        rot_base = sb("rot_base", [P, 4, T])
        rselb = sb("rselb", [P, UNITS, P], BF16)
        rdselb = sb("rdselb", [P, PAIRS, P], BF16)
        onehot = sb("onehot", [H, H, P], BF16)
        ident_b = sb("ident_b", [P, P], BF16)
        mask_tb = sb("mask_tb", [P, QW + P], BF16)
        mask_sb = sb("mask_sb", [P, 2 * QW], BF16)
        zeros = sb("zeros", [P, 1, T])
        x1 = sb("x1", [P, B, T])
        xs = sb("xs", [P, B, T + 1])
        xw_sb = sb("xw_sb", [P, 4, P])
        xv = sb("xv", [P, 6])
        gates = sb("gates", [P, 2])
        big = sb("big", [P, BIG])
        used = [0]

        def view(cols, *shape, dt=F32):
            a = big[:, used[0]:used[0] + cols]
            used[0] += cols
            if dt == BF16:
                a = a.bitcast(BF16)
            names = "abcd"[:len(shape)]
            return a.rearrange(f"p ({' '.join(names)}) -> p {' '.join(names)}", **dict(zip(names, shape)))

        xtok = view(2 * P, NT, P)
        ctok = view(2 * P, NT, P)
        xhat = view(2 * P, NT, P)
        bst = sb("bst", [P, NT, 6])
        bag = sb("bag", [P, NT, 2])
        tv = sb("tv", [P, 5, NT])
        xhT = view(T, 1, T)[:, 0, :]
        cT = view(T, 1, T)[:, 0, :]
        qT = view(T, 1, T)[:, 0, :]
        kT = view(T, 1, T)[:, 0, :]
        kS = view(T, 1, T)[:, 0, :]
        vS = view(T, 1, T)[:, 0, :]
        kTb = view(T // 2, 1, T, dt=BF16)[:, 0, :]
        qpad = view(H * T, H, T)
        qpadb = view(H * T // 2, H, T, dt=BF16)
        vpad = view(NT * H * 32, NT, H, 32)
        xP = view(8 * 2 * T, 8, 2, T)
        xrd = view(T, 1, T)[:, 0, :]
        xo = view(T, 1, T)[:, 0, :]
        xo2 = view(T, 1, T)[:, 0, :]
        xproj = view(T, 1, T)[:, 0, :]
        stage_sel = view((UNITS + PAIRS) * P, UNITS + PAIRS, P)
        stage_hot = view(H * P, H, P)
        assert used[0] <= BIG
        used[0] = 0
        xc0 = view(CH * CW, CH, CW)
        sq0 = view(CH * CW, CH, CW)
        va0 = view(CH * CW, CH, CW)
        z0 = view(CH * CW, CH, CW)
        z1 = view(CH * CW, CH, CW)
        assert used[0] <= BIG
        used[0] = 0
        one = lambda: view(T, 1, T)[:, 0, :]
        sT = one()
        sq = view(8 * T, 8, T)
        qs = view(8 * T, 8, T)
        qp = view(8 * T, 8, T)
        rot = view(UNITS * T, UNITS, T)
        hat = view(UNITS * T, UNITS, T)
        hatb = view(UNITS * T // 2, UNITS, T, dt=BF16)
        vs = view(NT * INNER, NT, INNER)
        pt = view(8 * (QW + P), 8, QW + P)
        osb = view(PAIRS * T, PAIRS, T)
        n_s, n_y, n_t, n_r, n_z = one(), one(), one(), one(), one()
        d_s, d_y, d_t, d_r, d_z = one(), one(), one(), one(), one()
        half = lambda: view(T // 2, 1, T, dt=BF16)[:, 0, :]
        n_hi, n_mid, n_parts, d_hi, d_mid, d_parts = half(), half(), half(), half(), half(), half()
        s2, xc, sq2, va, y0, y1, xn = one(), one(), one(), one(), one(), one(), one()
        gt = view(3 * T, 3, T)
        a2 = one()
        assert used[0] <= BIG
        used[0] = 0
        otok = view(2 * 2 * P, 2, 2, P)

        mcol = sb("mcol", [P, NT, H])
        mrow = sb("mrow", [H, QW + P], BF16)
        tab = sb("tab", [P, 4, T])
        vecs = sb("vecs", [P, L, NV])
        va_c = sb("va_c", [P, 4])
        vf = sb("vf", [P, NV])
        wn_sb = sb("wn_sb", [P, 3 * INNER])
        wo_sb = sb("wo_sb", [P, PAIRS, P])
        w1_sb = sb("w1_sb", [P, 2 * HID])
        w2_sb = sb("w2_sb", [P, 3, P])
        ps = st.enter_context(nc.psum_tensor("ps", [P, 8, 512], F32))

        s_first, s_const, s_w, s_wo, s_wf, s_x = (sem(n) for n in ("s_first", "s_const", "s_w", "s_wo", "s_wf", "s_x"))
        s_out = [sem("s_out0"), sem("s_out1")]
        cast, gate, zero = sem("cast"), sem("gate"), sem("zero")
        xst, xln, xhat_d, xtr, xev, xpr, xqk, xvp, xpad, xpadb, xs_d, xmax = (
            sem(n) for n in ("xst", "xln", "xhat_d", "xtr", "xev", "xpr", "xqk", "xvp", "xpad", "xpadb", "xs_d", "xmax"))
        xv_d, xkb, xkt, xchain = sem("xv_d"), sem("xkb"), sem("xkt"), sem("xchain")
        xpad2 = sem("xpad2")
        xmt, xmr, xsc, xex, xav, xrd_d, xo_d, xwo, xres = (
            sem(n) for n in ("xmt", "xmr", "xsc", "xex", "xav", "xrd_d", "xo_d", "xwo", "xres"))
        turned = sem("turned")
        qev, swapped = sem("qev"), [sem("swapped0"), sem("swapped1")]
        vcur, tabs, shifted, proj, sq_d, vev, rotm, radd, sums, ss_d, ln_d, y_d, r_d = (
            sem(n) for n in ("vcur", "tabs", "shifted", "proj", "sq_d", "vev", "rotm", "radd", "sums", "ss_d", "ln_d", "y_d", "r_d"))
        rb, hat_d, hatb_d, sc_d, max_d, mt_d, mr_d = (
            sem(n) for n in ("rb", "hat_d", "hatb_d", "sc_d", "max_d", "mt_d", "mr_d"))
        st_d, ex_d, ov_d, oev, dev, dln, dy, dp, rdb, on_d, wo_d, x_d = (
            sem(n) for n in ("st_d", "ex_d", "ov_d", "oev", "dev", "dln", "dy", "dp", "rdb", "on_d", "wo_d", "x_d"))
        chain, nchain, nmid, dchain = sem("chain"), sem("nchain"), sem("nmid"), sem("dchain")
        nmean, nxc, nsq, nvar, nva, nln, ny, nxn, nt = (
            sem(n) for n in ("nmean", "nxc", "nsq", "nvar", "nva", "nln", "ny", "nxn", "nt"))
        fsh, fmean, fxc, fsq, fvar, fva, fln, fy, fchain, fxn = (
            sem(n) for n in ("fsh", "fmean", "fxc", "fsq", "fvar", "fva", "fln", "fy", "fchain", "fxn"))
        fh, fev, fg, fu, fo, fx, fvc = (sem(n) for n in ("fh", "fev", "fg", "fu", "fo", "fx", "fvc"))
        gx, tr_o, ev_o = sem("gx"), sem("tr_o"), sem("ev_o")

        xv_q, xv_k, xv_v, xv_o, g_x, g_f = (xv[:, i:i + 1] for i in range(6))
        CASTS = 6
        x_tok = x.rearrange("(b n p) d -> b p n d", b=B, p=P)
        c_tok = ctx_in.rearrange("(b n p) d -> b p n d", b=B, p=P)
        o_tok = out.rearrange("(b n p) d -> b p n d", b=B, p=P)
        hd = [4 * (i % 4) + i // 4 for i in range(H)]

        ORDER = [*range(0, 4), *range(8, 12), *range(4, 8), *range(12, 16)]
        place = {u: n for n, u in enumerate(ORDER)}
        ROW_BANK = [3] * 4 + [0, 1] * 2 + [3, 4] * 4
        POOL_TURNS = (2, 3)
        WHOLE = 3
        HATS = [i // 2 + PAIRS // 2 * (i % 2) for i in range(PAIRS)]
        PLAN = [(x_[0], int(x_[1:])) for x_ in """
            k0 h0 k1 h1 k2 h2 k3 h3 F1 w0 h4 g0 c0 h5 k4 F2 c1 w1 k5 n0 g1 h6 h7 F3 N0 k6 w2 h8 F4 h9 w3 R0
            R1 H0 h10 H1 b0 h11 b1 k7 w4 c2 F5 R2 h12 S0 g2 X0 H2 R3 S1 X1 H3 h13 V0 b2 S2 b3 v0 X2 V1 S3 X3
            w5 F6 g3 v1 h14 S4 n1 S5 S6 X4 X5 h15 N1 S7 w6 X6 F7 R4 H4 b4 w7 R5 R6 c3 X7 e0 H5 R7 b5 H6 E0
            b6 H7 b7 S8 S9 V2 E1 X8 E2 v2 X9 E3 S10 S11 V3 E4 X10 X11 S12 E5 X12 S13 X13 D0 v3 D1 Y0 Y1 S14
            S15 X14 X15 D2 D3 O0 O1 Y2 O2 Y3 O3 M0 m0 O4 O5 O6 O7""".split()]

        def share(A, Bh, F):
            return [x_ for x_ in PLAN if x_[0] in "kgnNcRHbSXVvMm" * A + "hweEDYO" * Bh + "F" * F]

        def cross(eng, body):
            body(0, True, False)
            with eng.Fori(1, B) as b:
                body(b, True, True)
            body(B, False, True)

        def seq(b, n):
            return slice((b - n) % B, (b - n) % B + 1) if isinstance(b, int) else bass.ds(b - n, 1)

        def pipeline(eng, body, layer_start=None, layer_second=None):
            def layer(l, first):
                if layer_start:
                    layer_start(l, first)
                body(0, eng.snap(l * B) if not first else 0, l, True, not first, not first, first)
                body(1, eng.snap(l * B + 1) if not first else 1, l, True, True, not first, first)
                if layer_second:
                    layer_second(l, first)
                with eng.Fori(2, B) as b:
                    body(b, eng.snap(l * B + b), l, True, True, True, first)
            layer(0, True)
            with eng.Fori(1, L) as l:
                layer(l, False)
            body(0, L * B, L, False, True, True, False)
            body(1, L * B + 1, L, False, False, True, False)

        block = st.enter_context(nc.Block())

        @block.sync
        def _(eng):
            eng.dma_start(xtok, x_tok[0]).then_inc(s_x, 16)
            eng.dma_start(sel[:, :], c_sel).then_inc(s_first, 16)
            eng.dma_start(ctok, c_tok[0]).then_inc(s_x, 16)
            eng.dma_start(xw_sb[:, :, :], xw).then_inc(s_first, 16)
            eng.dma_start(xv[:, :], xvec).then_inc(s_first, 16)
            eng.dma_start(stage_hot[0:H].rearrange("h a b -> h (a b)"), c_onehot).then_inc(s_const, 16)
            eng.dma_start(stage_sel.rearrange("p a b -> p (a b)"), c_rsel).then_inc(s_const, 16)
            eng.dma_start(rot_base[:, :, :].rearrange("p a b -> p (a b)"), c_rot).then_inc(s_const, 16)
            eng.dma_start(vecs[:, :, :], vec).then_inc(s_const, 16)
            with eng.Fori(1, B) as b:
                eng.wait_ge(xtr, b * 6 + FREE)
                eng.dma_start(xtok, x_tok[bass.ds(b, 1)].rearrange("a p n d -> p (a n) d")).then_inc(s_x, 16)
                eng.dma_start(ctok, c_tok[bass.ds(b, 1)].rearrange("a p n d -> p (a n) d")).then_inc(s_x, 16)

            def swaps(it):
                for g in range(4):
                    eng.wait_ge(qev, it * PAIRS + (2 * g + 2))
                    cols_ = slice(4 * (g % 2), 4 * (g % 2) + 4)
                    for r in range(4):
                        r2 = r ^ 1
                        eng.dma_start(qp[32 * r2:32 * r2 + 32, cols_, :], qs[32 * r:32 * r + 32, cols_, :]).then_inc(swapped[g % 2], 16)

            def load_up(l):
                src = lambda w: w[0:1] if isinstance(l, int) else w[bass.ds(l, 1)]
                eng.dma_start(w1_sb[:, :], src(w1).rearrange("a p n -> p (a n)")).then_inc(s_wf, 16)
                eng.dma_start(w2_sb[:, :, :], src(w2).rearrange("a p j n -> p (a j) n")).then_inc(s_wf, 16)

            eng.dma_start(wn_sb[:, :], wn[0:1].rearrange("a p n -> p (a n)")).then_inc(s_w, 16)
            eng.dma_start(wo_sb[:, :, :], wo[0:1].rearrange("a p j n -> p (a j) n")).then_inc(s_wo, 16)
            load_up(0)
            with eng.Fori(0, B) as b:
                swaps(eng.snap(b + 0))
            with eng.Fori(1, L) as l:
                eng.wait_ge(proj, l * (B * (PAIRS + 4)) + FREE)
                eng.dma_start(wn_sb[:, :], wn[bass.ds(l, 1)].rearrange("a p n -> p (a n)")).then_inc(s_w, 16)
                swaps(eng.snap(l * B))
                eng.wait_ge(wo_d, l * B + FREE)
                eng.dma_start(wo_sb[:, :, :], wo[bass.ds(l, 1)].rearrange("a p j n -> p (a j) n")).then_inc(s_wo, 16)
                swaps(eng.snap(l * B + 1))
                eng.wait_ge(fo, l * B + FREE)
                load_up(l)
                with eng.Fori(2, B) as b:
                    swaps(eng.snap(l * B + b))
            for b in range(B):
                eng.wait_ge(ev_o, b + 1)
                eng.dma_start(o_tok[b], otok[:, b % 2, :, :]).then_inc(s_out[b % 2], 16)
            for q in s_out:
                eng.wait_ge(q, 16 * (B // 2))

        @block.gpsimd
        def _(eng):
            eng.sem_inc(radd, FREE)
            eng.memset(vpad, 0.0).then_inc(zero, 1)
            eng.memset(xs[:, :, 0:1], 0.0).then_inc(zero, 1)
            eng.memset(zeros[:, :, :], 0.0).then_inc(zero, 1)
            eng.wait_ge(s_first, 16 * 3)
            eng.wait_ge(s_const, 16 * 4)
            eng.tensor_copy(ident_b[:, :], ident).then_inc(cast, 1)
            eng.tensor_copy(mask_tb[:, :], part["mask_t"]).then_inc(cast, 1)
            eng.tensor_copy(mask_sb[:, :], part["mask_s"]).then_inc(cast, 1)
            eng.tensor_copy(onehot[:, :, :], stage_hot[0:H]).then_inc(cast, 1)
            eng.tensor_copy(rselb[:, :, :], stage_sel[:, 0:UNITS, :]).then_inc(cast, 1)
            eng.tensor_copy(rdselb[:, :, :], stage_sel[:, UNITS:UNITS + PAIRS, :]).then_inc(cast, 1)
            eng.wait_ge(nxn, CH)
            eng.memset(gt[:, 2, :], 0.0).then_inc(zero, 1)
            eng.wait_ge(zero, 4)

            def body(b, it, l, A, Bh, F, first):
                def copy(dst, src, rows):
                    if isinstance(b, int):
                        return eng.tensor_tensor(dst, src, zeros[rows, :, :], ALU.add)
                    return eng.tensor_copy(dst, src)

                if A:
                    if not first:
                        eng.wait_ge(fx, it + (1 - B) + FREE)
                    eng.wait_ge(proj, it * (PAIRS + 4) + FREE)
                    eng.wait_ge(radd, it * UNITS + FREE)
                    for rows, off in ((slice(0, 64), 1), (slice(64, P), 0)):
                        copy(sT[rows, :].rearrange("p (a t) -> p a t", a=1), xs[rows, seq(b, 0), off:off + T], rows).then_inc(shifted, 1)
                if F:
                    eng.wait_ge(fxc, it - 2 + FREE)
                    eng.wait_ge(x_d, it - 1 + FREE)
                    for rows, off in ((slice(0, 64), 1), (slice(64, P), 0)):
                        copy(s2[rows, :].rearrange("p (a t) -> p a t", a=1), xs[rows, seq(b, 2), off:off + T], rows).then_inc(fsh, 1)
                if A:
                    eng.wait_ge(shifted, it * 2 + 2)
                    if F:
                        eng.wait_ge(fsh, it * 2 - 2)
                    eng.wait_ge(hat_d, it * PAIRS + FREE)
                    for g in range(4):
                        if g in POOL_TURNS:
                            eng.wait_ge(swapped[g % 2], it * 128 + (g // 2 * 64 + 64))
                            eng.wait_ge(tabs, l * 4 + 4)
                            for n in range(4 * g, 4 * g + 4):
                                k = ORDER[n] // PAIRS
                                eng.tensor_tensor(qp[:, n % 8, :], qp[:, n % 8, :], tab[:, 2 * k + 1, :], ALU.mult).then_inc(turned, 1)
                                if g == WHOLE:
                                    eng.tensor_tensor(qs[:, n % 8, :], qs[:, n % 8, :], tab[:, 2 * k, :], ALU.mult).then_inc(turned, 1)
                        for n in range(4 * g, 4 * g + 4):
                            if g == WHOLE:
                                eng.wait_ge(turned, it * 12 + 12)
                            else:
                                if g in POOL_TURNS:
                                    eng.wait_ge(turned, it * 12 + 4)
                                eng.wait_ge(rotm, it * 12 + n + 1)
                            eng.tensor_tensor(rot[:, ORDER[n], :], qs[:, n % 8, :], qp[:, n % 8, :], ALU.add).then_inc(radd, 1)
            pipeline(eng, body)

        @block.scalar
        def _(eng):
            eng.sem_inc(oev, FREE)
            eng.sem_inc(mr_d, FREE)
            eng.sem_inc(xmr, FREE)
            eng.wait_ge(s_first, 16 * 3)
            eng.activation(gates[:, :], xv[:, 4:6], ACT.Tanh).then_inc(gate, 1)
            eng.preload_act_table_set("natural_log_exp_and_others")
            eng.wait_ge(zero, 3)

            def cross_body(b, X1, X2):
                def exps(pr):
                    for n in (2 * pr, 2 * pr + 1):
                        eng.wait_ge(xsc, b * H + (n + 1 - H))
                        if n >= 8:
                            eng.wait_ge(xav, b * 4 + ((n - 8) // 4 + 1 - 4))
                        eng.activation(xP[:, n % 8, :, :], ps[:, 2 + n % 4, :].rearrange("p (a t) -> p a t", a=2),
                                       ACT.Exp).then_inc(xex, 1)

                for pr in range(PAIRS):
                    if X1 and pr == 0:
                        x1b = x1[:, b, :] if isinstance(b, int) else x1[:, bass.ds(b, 1), :].rearrange("p a t -> p (a t)")
                        eng.wait_ge(xtr, b * 6 + (2 + FREE))
                        eng.activation(x1b, ps[:, 0, 0:T], ACT.Copy).then_inc(xev, 1)
                        eng.wait_ge(xtr, b * 6 + (4 + FREE))
                        eng.activation(cT, ps[:, 1, 0:T], ACT.Copy).then_inc(xev, 1)
                        eng.wait_ge(xst, b + 1)
                        eng.activation(tv[:, 1, :], tv[:, 0, :], ACT.Ln).then_inc(xln, 1)
                        eng.wait_ge(xln, b * 2 + 1)
                        eng.activation(tv[:, 2, :], tv[:, 1, :], ACT.Exp, scale=-0.5).then_inc(xln, 1)
                    if X2:
                        exps(pr)
                    if X1 and pr == 1:
                        eng.wait_ge(xtr, b * 6 + (6 + FREE))
                        eng.activation(xhT, ps[:, 0, 0:T], ACT.Copy).then_inc(xev, 1)
                    if X1 and pr == 2:
                        eng.wait_ge(xqk, b * 2 + 2)
                        eng.activation(kTb, kS, ACT.Copy).then_inc(xkb, 1)
                if X1:
                    for i in range(H // 2, H):
                        eng.activation(qpad[:, i, :], qT, ACT.Copy, scale=hmask[:, hd[i]:hd[i] + 1]).then_inc(xpad2, 1)
                    eng.activation(kT, kS, ACT.Copy).then_inc(xkt, 1)
                    eng.wait_ge(xmt, b + 1)
                    eng.activation(mrow[:, 0:T], ps[0:H, 0, 0:T], ACT.Copy).then_inc(xmr, 1)

            cross(eng, cross_body)

            for c in range(CH):
                eng.wait_ge(nxc, c + 1)
                eng.activation(sq0[:, c, :], xc0[:, c, :], ACT.Square).then_inc(nsq, 1)
            for c in range(CH):
                eng.wait_ge(nva, c + 1)
                eng.activation(z0[:, c, :], va0[:, c, :], ACT.Ln).then_inc(nln, 1)
            for c in range(CH):
                eng.wait_ge(nln, c + 1)
                eng.activation(z0[:, c, :], z0[:, c, :], ACT.Exp, scale=-0.5).then_inc(ny, 1)

            def body(b, it, l, A, Bh, F, first):
                for kind, i in share(A, Bh, F):
                    if kind == "k":
                        two = slice(2 * (i % 4), 2 * (i % 4) + 2)
                        bank = ps[:, i % 2, :].rearrange("p (a t) -> p a t", a=2)
                        eng.wait_ge(proj, it * (PAIRS + 4) + (i + 1 + FREE))
                        if i >= 4:
                            eng.wait_ge(sums, it * UNITS + (2 * i - 6 + FREE))
                        eng.activation(sq[:, two, :], bank, ACT.Square).then_inc(sq_d, 1)
                        if i % 2 == 0:
                            eng.wait_ge(radd, it * UNITS + (max(0, 2 * i - 4) + FREE))
                        eng.activation(qs[:, two, :], bank, ACT.Copy).then_inc(qev, 1)
                    if kind == "h":
                        eng.wait_ge(st_d, it * H + (i + 1 - H))
                        if i >= 8:
                            eng.wait_ge(ov_d, it * PAIRS + (2 * ((i - 8) // 4) + 2 - PAIRS))
                        eng.activation(pt[:, i % 8, :], ps[:, 5 + i % 2, 0:QW + P], ACT.Exp).then_inc(ex_d, 1)
                    if kind == "w":
                        eng.wait_ge(ov_d, it * PAIRS + (i + 1 - PAIRS))
                        eng.activation(osb[:, i, :], ps[:, 7, 0:T], ACT.Copy).then_inc(oev, 1)
                    if kind == "n":
                        eng.wait_ge(ss_d, it * 2 + (i + 1))
                        eng.activation(n_t, n_s, ACT.Ln).then_inc(ln_d, 1)
                        eng.wait_ge(ln_d, it * 2 + (i + 1))
                        eng.activation(n_y, n_t, ACT.Exp, scale=-0.5).then_inc(y_d, 1)
                    if kind == "b":
                        two = slice(2 * HATS[i], 2 * HATS[i] + 2)
                        eng.wait_ge(hat_d, it * PAIRS + (i + 1 + FREE))
                        eng.activation(hatb[:, two, :], hat[:, two, :], ACT.Copy).then_inc(hatb_d, 1)
                    if kind == "v":
                        n, c = i % 2, i // 2
                        eng.wait_ge(proj, it * (PAIRS + 4) + (PAIRS + i + 1 + FREE))
                        if Bh:
                            eng.wait_ge(ov_d, it * PAIRS + (4 * c + 4 - PAIRS))
                        eng.activation(vs[:, n, c * 512:c * 512 + 512], ps[:, i % 2, :], ACT.Copy).then_inc(vev, 1)
                    if kind == "m":
                        eng.wait_ge(mt_d, it + 1)
                        eng.activation(mrow[:, 0:QW], ps[0:H, 2, 0:QW], ACT.Copy).then_inc(mr_d, 1)
                        eng.activation(mrow[:, QW:QW + P], ps[0:H, 2, P:T], ACT.Copy).then_inc(mr_d, 1)
                    if kind == "e":
                        eng.wait_ge(dev, it)
                        eng.activation(d_t, d_s, ACT.Ln).then_inc(dln, 1)
                        eng.wait_ge(dln, it)
                        eng.activation(d_y, d_t, ACT.Exp, scale=-1.0).then_inc(dy, 1)
                    if kind == "F" and i == 1:
                        eng.wait_ge(fxc, it - 1 + FREE)
                        eng.activation(sq2, xc, ACT.Square).then_inc(fsq, 1)
                    if kind == "F" and i == 2:
                        eng.wait_ge(fva, it - 1)
                        eng.activation(y1, va, ACT.Ln).then_inc(fln, 1)
                        eng.wait_ge(fln, it - 1)
                        eng.activation(y0, y1, ACT.Exp, scale=-0.5).then_inc(fy, 1)
                    if kind == "F" and i == 5:
                        eng.wait_ge(fev, it * 4 - 4)
                        eng.activation(gt, gt, ACT.Gelu).then_inc(fg, 1)
                        eng.preload_act_table_set("natural_log_exp_and_others")

            pipeline(eng, body)
            for b in range(B):
                eng.wait_ge(tr_o, b + 1)
                if b >= 2:
                    eng.wait_ge(s_out[b % 2], 16 * (b // 2))
                eng.activation(otok[:, b % 2, :, :], ps[:, b % 2, 0:T].rearrange("p (n d) -> p n d", n=NT),
                               ACT.Copy).then_inc(ev_o, 1)

        @block.vector
        def _(eng):
            for s in (hat_d, xres, on_d, fx, fxc, x_d):
                eng.sem_inc(s, FREE)
            eng.wait_ge(s_first, 16 * 3)
            eng.wait_ge(zero, 3)

            def cross_body(b, X1, X2):
                if X1:
                    eng.wait_ge(s_x, b * 32 + 32)
                    for n in range(NT):
                        eng.bn_stats(bst[:, n, :], xtok[:, n, :]).then_inc(chain, 1)
                    PER = 11
                    base = lambda c: b * PER + c
                    eng.wait_ge(chain, base(2))
                    eng.tensor_tensor(tv[:, 1, :], bst[:, :, 1], bst[:, :, 4], ALU.subtract).then_inc(chain, 1)
                    eng.tensor_tensor(tv[:, 2, :], bst[:, :, 2], bst[:, :, 5], ALU.add).then_inc(chain, 1)
                    eng.tensor_tensor(bag[:, 1, :], bst[:, :, 1], bst[:, :, 4], ALU.add).then_inc(chain, 1)
                    eng.wait_ge(chain, base(5))
                    eng.scalar_tensor_tensor(tv[:, 1, :], tv[:, 1, :], 0.25, tv[:, 1, :], ALU.mult, ALU.mult).then_inc(chain, 1)
                    eng.tensor_scalar(tv[:, 2, :], tv[:, 2, :], 1.0 / P, EPS, ALU.mult, ALU.add).then_inc(chain, 1)
                    eng.tensor_scalar(bag[:, 0, :], bag[:, 1, :], 0.5, None, ALU.mult).then_inc(chain, 1)
                    eng.wait_ge(chain, base(8))
                    eng.tensor_tensor(tv[:, 0, :], tv[:, 1, :], tv[:, 2, :], ALU.add).then_inc(xst, 1)
                    eng.wait_ge(xln, b * 2 + 2)
                    eng.tensor_tensor(tv[:, 3, :], tv[:, 2, :], tv[:, 2, :], ALU.mult).then_inc(chain, 1)
                    eng.wait_ge(chain, base(9))
                    eng.scalar_tensor_tensor(tv[:, 3, :], tv[:, 3, :], -0.5, tv[:, 0, :], ALU.mult, ALU.mult).then_inc(chain, 1)
                    eng.wait_ge(chain, base(10))
                    eng.scalar_tensor_tensor(tv[:, 4, :], tv[:, 3, :], 1.5, tv[:, 2, :], ALU.add, ALU.mult).then_inc(chain, 1)
                    eng.wait_ge(chain, base(11))
                    for n in range(NT):
                        eng.tensor_scalar(xhat[:, n, :], xtok[:, n, :], bag[:, 0, n:n + 1], tv[:, 4, n:n + 1],
                                          ALU.subtract, ALU.mult).then_inc(xhat_d, 1)
                    eng.wait_ge(xpr, b * 4 + 2)
                    eng.tensor_scalar(qT, ps[:, 1, 0:T], xv_q, float(np.float32(1) / np.sqrt(np.float32(XD))),
                                      ALU.add, ALU.mult).then_inc(xqk, 1)
                    eng.tensor_scalar(kS, ps[:, 1, T:2 * T], xv_k, None, ALU.add).then_inc(xqk, 1)
                    eng.wait_ge(xpr, b * 4 + 4)
                    eng.tensor_copy(vS, ps[:, 0, 0:T]).then_inc(xv_d, 1)
                    eng.wait_ge(xqk, b * 2 + 1)
                    for i in range(H):
                        eng.tensor_scalar(qpadb[:, i, :], qT, hmask[:, hd[i]:hd[i] + 1], None, ALU.mult).then_inc(xpadb, 1)
                    for n in range(NT * PAIRS):
                        t_, pr = divmod(n, PAIRS)
                        eng.wait_ge(xs_d, b * (NT * PAIRS) + (n + 1))
                        eng.tensor_reduce(mcol[:, t_, 2 * pr:2 * pr + 2], ps[:, n % 2, :].rearrange("p (a t) -> p a t", a=2),
                                          AX.X, ALU.max, negate=True).then_inc(xmax, 1)
                    if X2:
                        eng.wait_ge(xsc, b * H)
                    for i in range(H // 2):
                        eng.tensor_scalar(qpad[:, i, :], qT, hmask[:, hd[i]:hd[i] + 1], None, ALU.mult).then_inc(xpad, 1)
                if X2:
                    eng.wait_ge(xav, b * 4)
                    eng.reciprocal(xrd, ps[:, 7, 0:T]).then_inc(xrd_d, 1)
                    eng.wait_ge(xrd_d, b)
                    eng.tensor_tensor(xo, ps[:, 6, 0:T], xrd, ALU.mult).then_inc(xchain, 1)
                    eng.wait_ge(xchain, b * 2 - 1)
                    eng.tensor_scalar(xo2, xo, xv_v, None, ALU.add).then_inc(xo_d, 1)
                if X1:
                    eng.wait_ge(xv_d, b + 1)
                    vsrc = vS.rearrange("p (n a j d) -> p n a j d", n=NT, a=4, j=4)
                    vdst = vpad.rearrange("p n (a j) (m d) -> p n a j m d", j=4, m=4)
                    for n in range(NT):
                        for j in range(4):
                            eng.tensor_copy(vdst[:, n, :, j, j, :], vsrc[:, n, :, j, :]).then_inc(xvp, 1)
                if X2:
                    eng.wait_ge(xwo, b)
                    eng.wait_ge(gate, 1)
                    eng.tensor_scalar(xproj, ps[:, 6, 0:T], xv_o, gates[:, 0:1], ALU.add, ALU.mult).then_inc(xchain, 1)
                    eng.wait_ge(xchain, b * 2)
                    x1b = x1[:, B - 1, :] if isinstance(b, int) else x1[:, bass.ds(b - 1, 1), :].rearrange("p a t -> p (a t)")
                    eng.tensor_tensor(x1b, x1b, xproj, ALU.add).then_inc(xres, 1)

            cross(eng, cross_body)

            eng.wait_ge(s_const, 16 * 4)
            for c in range(CH):
                eng.wait_ge(nmean, c + 1)
                eng.tensor_tensor(xc0[:, c, :], x1[:, 2 * c:2 * c + 2, :].rearrange("p a t -> p (a t)"), ps[:, c, :],
                                  ALU.subtract).then_inc(nxc, 1)
            for c in range(CH):
                eng.wait_ge(nvar, c + 1)
                eng.tensor_scalar(va0[:, c, :], ps[:, 4 + c, :], EPS, None, ALU.add).then_inc(nva, 1)
            for c in range(CH):
                eng.wait_ge(ny, c + 1)
                eng.tensor_tensor(z1[:, c, :], z0[:, c, :], z0[:, c, :], ALU.mult).then_inc(nt, 1)
            for c in range(CH):
                eng.wait_ge(nt, c + 1)
                eng.scalar_tensor_tensor(z1[:, c, :], z1[:, c, :], -0.5, va0[:, c, :], ALU.mult, ALU.mult).then_inc(nt, 1)
            for c in range(CH):
                eng.wait_ge(nt, CH + c + 1)
                eng.scalar_tensor_tensor(z1[:, c, :], z1[:, c, :], 1.5, z0[:, c, :], ALU.add, ALU.mult).then_inc(nt, 1)
            for c in range(CH):
                eng.wait_ge(nt, 2 * CH + c + 1)
                eng.tensor_tensor(xs[:, 2 * c:2 * c + 2, 1:T + 1], xc0[:, c, :].rearrange("p (a t) -> p a t", a=2),
                                  z1[:, c, :].rearrange("p (a t) -> p a t", a=2), ALU.mult).then_inc(nxn, 1)

            def layer_start(l, first):
                src = vecs[:, 0, 0:4] if first else vecs[:, bass.ds(l, 1), 0:4].rearrange("p a n -> p (a n)")
                if not first:
                    eng.wait_ge(radd, l * (B * UNITS) + FREE)
                eng.tensor_copy(va_c[:, :], src).then_inc(vcur, 1)
                eng.wait_ge(vcur, l + 1)
                for i in range(4):
                    eng.tensor_scalar(tab[:, i, :], rot_base[:, i, :], va_c[:, i:i + 1], None, ALU.mult).then_inc(tabs, 1)

            def layer_second(l, first):
                src = vecs[:, 0, :] if first else vecs[:, bass.ds(l, 1), :].rearrange("p a n -> p (a n)")
                eng.tensor_copy(vf[:, :], src).then_inc(fvc, 1)

            def body(b, it, l, A, Bh, F, first):
                def norm_ffn():
                    fb = lambda c: it * 4 + (c - 8)
                    eng.wait_ge(fy, it - 1)
                    eng.tensor_tensor(y1, y0, y0, ALU.mult).then_inc(fchain, 1)
                    eng.wait_ge(fchain, fb(1))
                    eng.scalar_tensor_tensor(y1, y1, -0.5, va, ALU.mult, ALU.mult).then_inc(fchain, 1)
                    eng.wait_ge(fchain, fb(2))
                    eng.scalar_tensor_tensor(y1, y1, 1.5, y0, ALU.add, ALU.mult).then_inc(fchain, 1)
                    eng.wait_ge(fchain, fb(3))
                    eng.tensor_tensor(xc, xc, y1, ALU.mult).then_inc(fchain, 1)
                    eng.wait_ge(fchain, fb(4))
                    eng.tensor_scalar(xn, xc, vf[:, 4:5], vf[:, 5:6], ALU.mult, ALU.add).then_inc(fxn, 1)

                def norm_heads(j):
                    eng.wait_ge(y_d, it * 2 + (j + 1))
                    nb = lambda c: it * 10 + (5 * j + c - 1)
                    eng.tensor_tensor(n_t, n_y, n_y, ALU.mult).then_inc(nchain, 1)
                    eng.wait_ge(nchain, nb(2))
                    eng.scalar_tensor_tensor(n_t, n_t, -0.5, n_s, ALU.mult, ALU.mult).then_inc(nchain, 1)
                    eng.wait_ge(nchain, nb(3))
                    eng.scalar_tensor_tensor(n_r, n_t, 1.5, n_y, ALU.add, ALU.mult).then_inc(nchain, 1)
                    eng.wait_ge(nchain, nb(4))
                    eng.tensor_copy(n_hi, n_r).then_inc(nchain, 1)
                    eng.wait_ge(nchain, nb(5))
                    eng.scalar_tensor_tensor(n_z, n_hi, part["parts"][:, 0:1], n_r, ALU.mult, ALU.add).then_inc(nchain, 1)
                    eng.wait_ge(nchain, nb(6))
                    eng.tensor_copy(n_mid, n_z).then_inc(nmid, 1)
                    eng.wait_ge(nmid, it * 2 + (j + 1))
                    eng.scalar_tensor_tensor(n_parts, n_mid, part["parts"][:, 1:2], n_z, ALU.mult, ALU.add).then_inc(r_d, 1)

                def ffn(s):
                    f3 = it * 3 - 6
                    if s == 1:
                        eng.wait_ge(fmean, it - 1)
                        eng.wait_ge(fsh, it * 2 - 2)
                        eng.tensor_tensor(xc, s2, ps[:, 3, 0:T], ALU.subtract).then_inc(fxc, 1)
                    if s == 2:
                        eng.wait_ge(fvar, it - 1)
                        eng.tensor_scalar(va, ps[:, 3, 0:T], EPS, None, ALU.add).then_inc(fva, 1)
                    if s == 3:
                        norm_ffn()
                    if s == 4:
                        eng.wait_ge(fh, f3 + 1)
                        for j in range(2):
                            eng.tensor_scalar(gt[:, j, :], ps[:, 3, j * T:j * T + T], vf[:, 9 + j:10 + j], None,
                                              ALU.add).then_inc(fev, 1)
                    if s == 5:
                        m = HC[2][1]
                        eng.wait_ge(fh, f3 + 2)
                        eng.tensor_scalar(gt[0:m, 2, :], ps[0:m, 3, 0:T], vf[0:m, 11:12], None, ALU.add).then_inc(fev, 1)
                        eng.tensor_scalar(a2[0:m, :], ps[0:m, 3, T:2 * T], vf[0:m, 8:9], None, ALU.add).then_inc(fev, 1)
                    if s == 6:
                        m = HC[2][1]
                        eng.wait_ge(fh, f3 + 3)
                        eng.wait_ge(fg, it - 1)
                        for j in range(2):
                            eng.scalar_tensor_tensor(gt[:, j, :], ps[:, 3, j * T:j * T + T], vf[:, 6 + j:7 + j],
                                                     gt[:, j, :], ALU.add, ALU.mult).then_inc(fu, 1)
                        eng.tensor_tensor(gt[0:m, 2, :], a2[0:m, :], gt[0:m, 2, :], ALU.mult).then_inc(fu, 1)
                    if s == 7:
                        eng.wait_ge(fo, it - 1 + FREE)
                        xb = xs[:, seq(b, 2), 1:T + 1]
                        eng.scalar_tensor_tensor(xb, ps[:, 3:4, 0:T], vf[:, 12:13], xb, ALU.add, ALU.add).then_inc(fx, 1)

                if A:
                    eng.wait_ge(tabs, l * 4 + 4)
                if F:
                    eng.wait_ge(fvc, l if isinstance(b, int) else l + 1)
                for kind, i in share(A, Bh, F):
                    if kind == "n":
                        eng.wait_ge(sums, it * UNITS + (8 * i + 8 + FREE))
                        eng.tensor_scalar(n_s, ps[:, 2, i * T:i * T + T], 1e-24, 65536.0, ALU.max, ALU.mult).then_inc(ss_d, 1)
                    if kind == "N":
                        norm_heads(i)
                    if kind == "F":
                        ffn(i)
                    if kind == "c" and i != WHOLE:
                        eng.wait_ge(swapped[i % 2], it * 128 + (i // 2 * 64 + 64))
                        for n in range(4 * i, 4 * i + 4):
                            k = ORDER[n] // PAIRS
                            if i not in POOL_TURNS:
                                eng.tensor_tensor(qp[:, n % 8, :], qp[:, n % 8, :], tab[:, 2 * k + 1, :], ALU.mult)
                            eng.tensor_tensor(qs[:, n % 8, :], qs[:, n % 8, :], tab[:, 2 * k, :], ALU.mult).then_inc(rotm, 1)
                    if kind == "H":
                        two = slice(2 * HATS[i], 2 * HATS[i] + 2)
                        bank = (1, 0, 0, 1, 5, 6, 5, 6)[i]
                        eng.wait_ge(rb, it * PAIRS + (i + 1))
                        eng.wait_ge(radd, it * UNITS + (place[two.stop - 1] + 1 + FREE))
                        if Bh and i % 2 == 0:
                            eng.wait_ge(st_d, it * H + (2 * i + 4 - H))
                        eng.tensor_tensor(hat[:, two, :], rot[:, two, :], ps[:, bank, :].rearrange("p (a t) -> p a t", a=2),
                                          ALU.mult).then_inc(hat_d, 1)
                    if kind == "X":
                        eng.wait_ge(sc_d, it * H + (i + 1))
                        eng.tensor_reduce(mcol[:, :, i:i + 1].rearrange("p a b -> p (a b)"),
                                          ps[:, ROW_BANK[i], 0:2 * QW].rearrange("p (a t) -> p a t", a=2), AX.X, ALU.max,
                                          negate=True).then_inc(max_d, 1)
                    if kind == "e":
                        eng.wait_ge(ov_d, it * PAIRS)
                        eng.tensor_copy(d_s, ps[:, 4, 0:T]).then_inc(dev, 1)
                    if kind == "E":
                        if i == 0:
                            eng.wait_ge(dy, it)
                            eng.tensor_tensor(d_t, d_s, d_y, ALU.mult).then_inc(dchain, 1)
                            continue
                        eng.wait_ge(dchain, it * 5 + (i - 5))
                        if i == 1:
                            eng.scalar_tensor_tensor(d_r, d_t, -2.0, d_y, ALU.add, ALU.mult).then_inc(dchain, 1)
                        if i == 2:
                            eng.tensor_copy(d_hi, d_r).then_inc(dchain, 1)
                        if i == 3:
                            eng.scalar_tensor_tensor(d_z, d_hi, part["parts"][:, 2:3], d_r, ALU.mult, ALU.add).then_inc(dchain, 1)
                        if i == 4:
                            eng.tensor_copy(d_mid, d_z).then_inc(dchain, 1)
                        if i == 5:
                            eng.scalar_tensor_tensor(d_parts, d_mid, part["parts"][:, 3:4], d_z, ALU.mult, ALU.add).then_inc(dp, 1)
                    if kind == "Y":
                        eng.wait_ge(rdb, it * 4 + (i + 1 - 4))
                        eng.wait_ge(oev, it * PAIRS + (2 * i + 2 - PAIRS + FREE))
                        eng.tensor_tensor(osb[:, 2 * i:2 * i + 2, :], osb[:, 2 * i:2 * i + 2, :],
                                          ps[:, i % 2, :].rearrange("p (a t) -> p a t", a=2), ALU.mult).then_inc(on_d, 1)
                if Bh:
                    eng.wait_ge(wo_d, it + FREE)
                    xb = xs[:, seq(b, 1), 1:T + 1]
                    eng.tensor_tensor(xb, xb, ps[:, 7:8, 0:T], ALU.add).then_inc(x_d, 1)

            pipeline(eng, body, layer_start, layer_second)
            eng.wait_ge(fx, L * B + FREE)
            for b in range(B):
                eng.scalar_tensor_tensor(x1[:, b, :], xs[:, b, 1:T + 1], gates[:, 1:2], x1[:, b, :], ALU.mult,
                                         ALU.add).then_inc(gx, 1)

        @block.tensor
        def _(eng):
            for s in (xtr, proj, sums, wo_d, fo):
                eng.sem_inc(s, FREE)
            eng.wait_ge(s_first, 16 * 3)

            def cross_body(b, X1, X2):
                def tokens():
                    eng.wait_ge(s_x, b * 32 + 32)
                    eng.wait_ge(xmr, b + FREE)
                    for n in range(NT):
                        eng.transpose(ps[:, 0, n * P:n * P + P], xtok[:, n, :], ident).then_inc(xtr, 1)
                    for n in range(NT):
                        eng.transpose(ps[:, 1, n * P:n * P + P], ctok[:, n, :], ident).then_inc(xtr, 1)

                def normed_tokens():
                    eng.wait_ge(xev, b * 3 + 1)
                    for n in range(NT):
                        eng.wait_ge(xhat_d, b * NT + (n + 1))
                        eng.transpose(ps[:, 0, n * P:n * P + P], xhat[:, n, :], ident).then_inc(xtr, 1)

                def projections():
                    eng.wait_ge(xev, b * 3 + 3)
                    eng.matmul(ps[:, 1, 0:T], xw_sb[:, 0, :], xhT, start=True, stop=True).then_inc(xpr, 1)
                    eng.matmul(ps[:, 1, T:2 * T], xw_sb[:, 1, :], cT, start=True, stop=True).then_inc(xpr, 1)
                    for n in range(NT):
                        eng.matmul(ps[:, 0, n * P:n * P + P], cT[:, n * P:n * P + P], xw_sb[:, 2, :],
                                   start=True, stop=True).then_inc(xpr, 1)

                def row_scores(first, last):
                    for n in range(first, last):
                        t_, pr = divmod(n, PAIRS)
                        if n == 0:
                            eng.wait_ge(xv_d, b + 1)
                            eng.wait_ge(xkb, b + 1)
                        if n >= 2:
                            eng.wait_ge(xmax, b * (NT * PAIRS) + (n - 1))
                        if t_ == 0:
                            eng.wait_ge(xpadb, b * H + (2 * pr + 2))
                        for a in range(2):
                            mm = eng.matmul(ps[:, n % 2, a * T:a * T + T], qpadb[:, 2 * pr + a, t_ * P:t_ * P + P], kTb,
                                            start=True, stop=True)
                        mm.then_inc(xs_d, 1)

                def score(n):
                    pr, kt = divmod(n, 2)
                    if n == 0:
                        eng.wait_ge(cast, CASTS)
                        eng.wait_ge(xkt, b)
                        eng.wait_ge(xpad, b * (H // 2))
                    if n == PAIRS:
                        eng.wait_ge(xpad2, b * (H // 2))
                    if n >= 4:
                        eng.wait_ge(xex, b * (2 * PAIRS) + (n - 3 - 2 * PAIRS))
                    bank = ps[:, 2 + n % 4, :]
                    eng.matmul(bank, kT[:, kt * P:kt * P + P], qpad[:, 2 * pr:2 * pr + 2, :].rearrange("p a t -> p (a t)"),
                               start=True, stop=False, skip_group_check=True)
                    if n == 0:
                        eng.wait_ge(xmr, b + FREE)
                    for a in range(2):
                        mm = eng.matmul(bank[:, a * T:a * T + T], onehot[:, 2 * pr + a, :], mrow[:, 0:T],
                                        start=False, stop=a == 1, skip_group_check=True)
                    mm.then_inc(xsc, 1)

                def weigh(q):
                    if q == 0:
                        eng.wait_ge(xvp, b * 8)
                        eng.wait_ge(xres, b - 1 + FREE)
                    eng.wait_ge(xex, b * (2 * PAIRS) + (4 * q + 4 - 2 * PAIRS))
                    for bank in (6, 7):
                        for kt in range(NT):
                            for i in range(4 * q, 4 * q + 4):
                                h = hd[i]
                                g = h // 4
                                w = vpad[:, kt, h, :] if bank == 6 else xones[:, h % 4, :]
                                mm = eng.matmul(ps[32 * g:32 * g + 32, bank, 0:T], w, xP[:, (2 * (i // 2) + kt) % 8, i % 2, :],
                                                start=q == 0 and kt == 0, stop=q == 3 and kt == 1, skip_group_check=True)
                    mm.then_inc(xav, 1)

                for pr in range(PAIRS):
                    if X1:
                        if pr == 0:
                            tokens()
                        elif pr == 1:
                            normed_tokens()
                        elif pr == 2:
                            projections()
                    for half in range(2):
                        if X1 and pr >= 3:
                            row_scores(*((0, 1), (1, 2), (2, 3), (3, 5), (5, 6), (6, 8), (8, 10), (10, 12), (12, 13), (13, 14))
                                       [2 * (pr - 3) + half])
                        if X2:
                            score(2 * pr + half)
                    if X2 and pr in (2, 4, 6):
                        weigh(pr // 2 - 1)
                if X1:
                    row_scores(14, 16)
                if X2:
                    weigh(3)
                if X1:
                    eng.wait_ge(xmax, b * (NT * PAIRS) + NT * PAIRS)
                    for n in range(NT):
                        mm = eng.transpose(ps[0:H, 0, n * P:n * P + P], mcol[:, n, :], ident)
                    mm.then_inc(xmt, 1)
                if X2:
                    eng.wait_ge(xo_d, b)
                    eng.matmul(ps[:, 6, 0:T], xw_sb[:, 3, :], xo2, start=True, stop=True).then_inc(xwo, 1)

            cross(eng, cross_body)

            eng.wait_ge(xres, B + FREE)
            for c in range(CH):
                eng.matmul(ps[:, c, :], mean_w, x1[:, 2 * c:2 * c + 2, :].rearrange("p a t -> p (a t)"),
                           start=True, stop=True).then_inc(nmean, 1)
            for c in range(CH):
                eng.wait_ge(nsq, c + 1)
                eng.matmul(ps[:, 4 + c, :], mean_w, sq0[:, c, :], start=True, stop=True).then_inc(nvar, 1)
            eng.wait_ge(nxn, CH)


            def body(b, it, l, A, Bh, F, first):
                if A:
                    eng.wait_ge(shifted, it * 2 + 2)
                    if isinstance(b, int) and b == 0:
                        eng.wait_ge(s_w, l * 16 + 16)
                    if Bh:
                        eng.wait_ge(vev, it * 4)
                        eng.wait_ge(on_d, it * 4 + (FREE - 4))

                def project(k):
                    if k >= 2:
                        eng.wait_ge(qev, it * PAIRS + (k - 1))
                    if k == 7:
                        eng.wait_ge(hat_d, it * PAIRS + (1 + FREE))
                    for a in range(2):
                        u = ORDER[2 * k + a]
                        mm = eng.matmul(ps[:, k % 2, a * T:a * T + T], wn_sb[:, u * P:u * P + P], sT, start=True, stop=True)
                    mm.then_inc(proj, 1)

                def head_sums(g):
                    if g == 0:
                        eng.wait_ge(mr_d, it * 2 + FREE)
                    if g == 2:
                        eng.wait_ge(ss_d, it * 2 + 1)
                    for n in range(4 * g, 4 * g + 4):
                        u = ORDER[n]
                        q = u % 4
                        eng.wait_ge(sq_d, it * PAIRS + (n // 2 + 1))
                        eng.matmul(ps[32 * q:32 * q + 32, 2, g // 2 * T:g // 2 * T + T], sumsel[:, u // 4, :], sq[:, n % 8, :],
                                   start=g % 2 == 0, stop=g % 2 == 1, skip_group_check=True).then_inc(sums, 1)

                def values(j):
                    n, c = j % 2, j // 2
                    if j < 2:
                        eng.wait_ge(hat_d, it * PAIRS + (3 + j + FREE))
                    else:
                        eng.wait_ge(max_d, it * H + (5 + j))
                    eng.matmul(ps[:, j % 2, :], sT[:, n * P:n * P + P], wn_sb[:, 2 * INNER + c * 512:2 * INNER + c * 512 + 512],
                               start=True, stop=True).then_inc(proj, 1)

                def score(h):
                    p, r = divmod(h, 2)
                    rows = slice(64 * r, 64 * r + 64)
                    if h >= 2:
                        eng.wait_ge(ex_d, it * H + (h - 1 - H))
                    elif A and h == 0:
                        eng.wait_ge(hat_d, it * PAIRS + FREE)
                    bank = ps[:, 5 + r, :]
                    eng.matmul(bank[:, 0:QW + P], ident_b[:, :], mask_tb[:, :], start=True, stop=False, skip_group_check=True)
                    if h == 0:
                        eng.wait_ge(mr_d, it * 2 + FREE)
                    eng.matmul(bank[:, 0:QW + P], onehot[:, h, :], mrow[:, :], start=False, stop=False, skip_group_check=True)
                    for n, (lo, w) in enumerate(((0, QW), (QW, P))):
                        mm = eng.matmul(bank[:, lo:lo + w], hat[rows, PAIRS + p, n * P:n * P + P], hat[rows, p, n * P:n * P + w],
                                        start=False, stop=n == 1, skip_group_check=True)
                    mm.then_inc(st_d, 1)

                def weigh(p):
                    eng.wait_ge(ex_d, it * H + (2 * p + 2 - H))
                    if p:
                        eng.wait_ge(oev, it * PAIRS + (p - PAIRS + FREE))
                    else:
                        eng.wait_ge(x_d, it - 1 + FREE)
                    for n, (lo, w) in enumerate(((0, QW), (QW, P))):
                        for r in range(2):
                            h = 2 * p + r
                            mm = eng.matmul(ps[64 * r:64 * r + 64, 7, n * P:n * P + w],
                                            vs[:, n, h * D:h * D + D], pt[:, h % 8, lo:lo + w],
                                            start=n == 0, stop=n == 1, skip_group_check=True)
                    if p % 2:
                        for n, (lo, w) in enumerate(((0, QW), (QW, P))):
                            for h in range(2 * p - 2, 2 * p + 2):
                                g = h % 4
                                mm = eng.matmul(ps[32 * g:32 * g + 32, 4, n * P:n * P + w], densel[:, h // 4, :],
                                                pt[:, h % 8, lo:lo + w], start=h < 4 and n == 0,
                                                stop=h >= 12 and n == 1, skip_group_check=True)
                    mm.then_inc(ov_d, 1)

                def ffn(s):
                    f4 = it * 4 - 8
                    def up(col, j, at, stop=True):
                        o, m = HC[j]
                        o += HID * (col == "gate")
                        return eng.matmul(ps[0:m, 3, at:at + T], w1_sb[:, o:o + m], xn, start=True, stop=True)
                    if s == 1:
                        eng.wait_ge(fsh, it * 2 - 2)
                        eng.matmul(ps[:, 3, 0:T], mean_w, s2, start=True, stop=True).then_inc(fmean, 1)
                    if s == 2:
                        eng.wait_ge(fsq, it - 1)
                        eng.matmul(ps[:, 3, 0:T], mean_w, sq2, start=True, stop=True).then_inc(fvar, 1)
                    if s == 4:
                        if not isinstance(b, int):
                            eng.wait_ge(s_wf, l * 32 + 32)
                        eng.wait_ge(fxn, it - 1)
                        up("gate", 0, 0)
                        up("gate", 1, T).then_inc(fh, 1)
                    if s == 5:
                        eng.wait_ge(fev, f4 + 2)
                        up("gate", 2, 0)
                        up("a", 2, T).then_inc(fh, 1)
                    if s == 6:
                        eng.wait_ge(fev, f4 + 4)
                        if A:
                            eng.wait_ge(max_d, it * H + 4)
                        up("a", 0, 0)
                        up("a", 1, T).then_inc(fh, 1)
                    if s == 7:
                        for j, (_, m) in enumerate(HC):
                            eng.wait_ge(fu, it * 3 + (3 - 6))
                            mm = eng.matmul(ps[:, 3, 0:T], w2_sb[0:m, j, :], gt[0:m, j, :], start=j == 0, stop=j == 2)
                        mm.then_inc(fo, 1)

                def spread(n):
                    if n == 4 and Bh:
                        eng.wait_ge(ex_d, it * H)
                    if n % 4 == 0:
                        eng.wait_ge(r_d, it * 2 + (n // 4 + 1))
                    if n in (0, 1, 3):
                        eng.wait_ge(qev, it * PAIRS + (6, 7, 0, 8)[n])
                    elif n in (2, 6, 7):
                        eng.wait_ge(hat_d, it * PAIRS + ({2: 2, 6: 5, 7: 6}[n] + FREE))
                    bank = (1, 0, 0, 1, 5, 6, 5, 6)[n]
                    for a in range(2):
                        mm = eng.matmul(ps[:, bank, a * T:a * T + T], rselb[:, 2 * HATS[n] + a, :], n_parts, start=True, stop=True)
                    mm.then_inc(rb, 1)

                def row_score(h):
                    p, r = divmod(h, 2)
                    rows = slice(64 * r, 64 * r + 64)
                    if r == 0:
                        eng.wait_ge(hatb_d, it * PAIRS + (2 * (p // 2) + 2))
                    if h in (1, 2, 3):
                        eng.wait_ge(max_d, it * H + h)
                    elif h in (4, 5):
                        eng.wait_ge(vev, it * 4 + (h - 3))
                    elif h in (6, 7) or h >= 10:
                        eng.wait_ge(max_d, it * H + (h - 1))
                    elif h == 0 and F:
                        eng.wait_ge(fev, it * 4 - 4)
                    elif h == 8 and F:
                        eng.wait_ge(fx, it - 1 + FREE)
                    elif h == 9 and Bh:
                        eng.wait_ge(dev, it)
                    bank = ps[:, ROW_BANK[h], :]
                    eng.matmul(bank[:, 0:2 * QW], ident_b[:, :], mask_sb[:, :], start=True, stop=False, skip_group_check=True)
                    eng.matmul(bank[:, WIN:QW], hatb[rows, p, 0:P], hatb[rows, PAIRS + p, 0:P], start=False, stop=False,
                               skip_group_check=True)
                    eng.matmul(bank[:, QW:2 * QW], hatb[rows, p, P:T], hatb[rows, PAIRS + p, P - WIN:T],
                               start=False, stop=True, skip_group_check=True).then_inc(sc_d, 1)

                def spread_reciprocals(i):
                    if i == 0:
                        eng.wait_ge(dp, it)
                    if i < 2 and A:
                        eng.wait_ge(vev, it * 4 + (3 + i))
                    if i >= 2:
                        eng.wait_ge(on_d, it * 4 + (i - 1 - 4 + FREE))
                    for a in range(2):
                        mm = eng.matmul(ps[:, i % 2, a * T:a * T + T], rdselb[:, 2 * i + a, :], d_parts, start=True, stop=True)
                    mm.then_inc(rdb, 1)

                def project_out(p):
                    if p == 0 and isinstance(b, int) and b == 1:
                        eng.wait_ge(s_wo, l * 16 + 16)
                    eng.wait_ge(on_d, it * 4 + (p // 2 + 1 - 4 + FREE))
                    mm = eng.matmul(ps[:, 7, 0:T], wo_sb[:, p, :], osb[:, p, :], start=p == 0, stop=p == PAIRS - 1)
                    if p == PAIRS - 1:
                        mm.then_inc(wo_d, 1)

                def transpose_maxima(_):
                    eng.wait_ge(max_d, it * H + H)
                    for n in range(NT):
                        mm = eng.transpose(ps[0:H, 2, n * P:n * P + P], mcol[:, n, :], ident)
                    mm.then_inc(mt_d, 1)

                steps = {"k": project, "g": head_sums, "V": values, "R": spread, "S": row_score, "M": transpose_maxima,
                         "h": score, "w": weigh, "D": spread_reciprocals, "O": project_out, "F": ffn}
                for kind, i in share(A, Bh, F):
                    if kind in steps:
                        steps[kind](i)

            pipeline(eng, body)
            for b in range(B):
                eng.wait_ge(gx, b + 1)
                if b >= 2:
                    eng.wait_ge(ev_o, b - 1)
                for n in range(NT):
                    mm = eng.transpose(ps[:, b % 2, n * P:n * P + P], x1[:, b, n * P:n * P + P], ident)
                mm.then_inc(tr_o, 1)


def laid_out(inputs):
    a = {k: np.asarray(v) for k, v in inputs.items()}
    up = "L0_xattn_"
    fp = "L0_ffn_"
    wn = a[fp + "Wqkv"]
    swap = (np.arange(D) + D // 2) % D
    two = lambda v: np.concatenate([v, v], 1)
    b1 = a[fp + "b1"]
    vec = np.zeros((P, L, NV), np.float32)
    qs, ks = a[fp + "q_scale"], a[fp + "k_scale"]
    for i, v in enumerate([two(qs), two(qs[:, swap]), two(ks), two(ks[:, swap]), a[fp + "ln_g"], a[fp + "ln_b"]]):
        vec[:, :, i] = v.T
    for j, (o, m) in enumerate(HC):
        vec[:m, :, 6 + j] = b1[:, o:o + m].T
        vec[:m, :, 9 + j] = b1[:, HID + o:HID + o + m].T
    vec[:, :, 12] = a[fp + "b2"].T
    w2 = np.zeros((L, P, 3, P), np.float32)
    for j, (o, m) in enumerate(HC):
        w2[:, :m, j, :] = a[fp + "W2"][:, o:o + m, :]
    xw = np.stack([a[up + n].T for n in ("Wq", "Wk", "Wv", "Wo")], 1)
    wide = lambda v: np.broadcast_to(v, (P,))
    xvec = np.stack([a[up + "bq"], a[up + "bk"], a[up + "bv"], a[up + "bo"], wide(a["g_xattn"]), wide(a["g_ffn"])], 1)
    arrays = {
        "x": a["x"].reshape(B * T, P), "ctx": a["ctx_1024"].reshape(B * T, P), "xw": xw, "xvec": xvec,
        "wn": wn, "wo": a[fp + "Wo"].reshape(L, PAIRS, P, P).transpose(0, 2, 1, 3), "w1": a[fp + "W1"],
        "w2": w2, "vec": vec,
    }
    arrays.update(shape_constants())
    return {k: np.ascontiguousarray(v) for k, v in arrays.items()}


def kernel(**inputs):
    import concourse.bacc as bacc
    from concourse.bass_utils import run_bass_kernel_spmd

    arrays = laid_out(inputs)
    nc = bacc.Bacc("TRN2", target_bir_lowering=False, num_devices=1)
    args = [nc.dram_tensor(f"in_{k}", v.shape, mybir.dt.from_np(v.dtype), kind="ExternalInput").ap()
            for k, v in arrays.items()]
    out = nc.dram_tensor("out_0", (B * T, P), F32, kind="ExternalOutput").ap()
    gated_flamingo(nc, *args, out)
    r = run_bass_kernel_spmd(nc, [{f"in_{k}": v for k, v in arrays.items()}], core_ids=[0])
    return r.results[0]["out_0"].reshape(B, T, P)
```
